# Optimizing a Trainium2 kernel written in Bass

```python
import numpy as np
import jax
import jax.numpy as jnp

def _softmax(x, axis=-1):
    return jax.nn.softmax(x, axis=axis)

def _gelu(x):
    return jax.nn.gelu(x, approximate=True)

def _silu(x):
    return jax.nn.silu(x)

def _sigmoid(x):
    return jax.nn.sigmoid(x)

def _layernorm(x, axis=-1, eps=1e-05):
    m = jnp.mean(x, axis=axis, keepdims=True)
    v = jnp.var(x, axis=axis, keepdims=True)
    return (x - m) / jnp.sqrt(v + eps)

def _scatter_add(tgt, idx, src, axis=0):
    return tgt.at[idx].add(src)

def _segment_sum(src, seg, n):
    return jax.ops.segment_sum(src, seg, n)
kernel_name = 'mk_decoder_postln_d1_seqx_r4_af255e'

def setup_inputs(seed: int=0):
    np.random.seed(seed)
    _w = jnp.asarray

    def _rec_inputs():
        import jax
        import jax.numpy as jnp
        _rk = jax.random.key(seed)
        x = 4.136e-05 + 0.9999 * jax.random.normal(jax.random.fold_in(_rk, 1), (4, 512, 512), jnp.float32)
        _lenS = 512 - jax.random.randint(jax.random.fold_in(_rk, 7), (4,), 0, max(1, 512 // 4) + 1, jnp.int32)
        _lenS2 = 512 - jax.random.randint(jax.random.fold_in(_rk, 8), (4,), 0, max(1, 512 // 4) + 1, jnp.int32)
        _ctx_1024P = jax.random.normal(jax.random.fold_in(_rk, 11), (4, 16, 256), jnp.float32)
        _ctx_1024c = jax.random.dirichlet(jax.random.fold_in(_rk, 511), 0.3 * jnp.ones((16,), jnp.float32), (4, 512))
        _ctx_1024t = jnp.einsum('bsk,bkd->bsd', _ctx_1024c, _ctx_1024P)
        _ctx_1024t = _ctx_1024t * jax.lax.rsqrt(jnp.mean(jnp.square(_ctx_1024t)) + 1e-12) * 0.953939
        ctx_1024 = -0.000292821 + 1.00034 * (_ctx_1024t + 0.3 * jax.random.normal(jax.random.fold_in(_rk, 611), (4, 512, 256), jnp.float32))
        return (x, ctx_1024)
    x, ctx_1024 = _rec_inputs()

    def _L0_attn_setup():
        import jax, jax.numpy as jnp
        import numpy as np
        HIDDEN = 512
        NUM_HEADS = 16
        NUM_KV_HEADS = 4
        HEAD_DIM = HIDDEN // NUM_HEADS
        Q_PER_KV = NUM_HEADS // NUM_KV_HEADS
        GROUP_SIZE = (Q_PER_KV + 2) * HEAD_DIM
        TOTAL_PROJ = NUM_KV_HEADS * GROUP_SIZE
        SEQ, BATCH = (512, 2)
        key = jax.random.key(seed)
        k1, k2, k3 = jax.random.split(key, 3)
        x = jax.random.normal(k1, (SEQ, BATCH, HIDDEN), dtype=jnp.float32)
        weight_qkv = jax.random.normal(k2, (TOTAL_PROJ, HIDDEN), dtype=jnp.float32) * 0.02
        weight_proj = jax.random.normal(k3, (HIDDEN, NUM_HEADS * HEAD_DIM), dtype=jnp.float32) * 0.02
        return {'x': x, 'weight_qkv': weight_qkv, 'weight_proj': weight_proj}
    _L0_attn_all = _L0_attn_setup()
    _L0_attn_in = {k: v for k, v in _L0_attn_all.items() if k in ('weight_qkv', 'weight_proj')}
    del _L0_attn_all

    def _L0_xattn_setup():
        import jax, jax.numpy as jnp
        import numpy as np
        import math
        B, L, DM = (2, 512, 256)
        DS, DC, EXP = (16, 4, 2)
        DI = EXP * DM
        DR = math.ceil(DM / 16)
        DT_MIN, DT_MAX, DT_FLOOR = (0.001, 0.1, 0.0001)

        def _ssm_forward(hidden_states, z, in_proj_w, conv_w, conv_b, x_proj_w, dt_proj_w, dt_proj_b, A_log, D):
            b = hidden_states.shape[0]
            x = jnp.einsum('ed,bld->bel', in_proj_w, hidden_states)
            xp = jnp.pad(x, ((0, 0), (0, 0), (DC - 1, 0)))
            xc = jax.lax.conv_general_dilated(xp, conv_w[:, None, :], window_strides=(1,), padding='VALID', dimension_numbers=('NCH', 'OIH', 'NCH'), feature_group_count=DI)
            u = jax.nn.silu(xc + conv_b[None, :, None])
            x_dbl = jnp.einsum('ke,bel->bkl', x_proj_w, u)
            dt_lo = x_dbl[:, :DR]
            Bm = x_dbl[:, DR:DR + DS]
            Cm = x_dbl[:, DR + DS:]
            delta = jax.nn.softplus(jnp.einsum('er,brl->bel', dt_proj_w, dt_lo) + dt_proj_b[None, :, None])
            A = -jnp.exp(A_log)

            def step(state, xs):
                d_t, B_t, C_t, u_t = xs
                dA = jnp.exp(d_t[..., None] * A)
                state = state * dA + (d_t * u_t)[..., None] * B_t[:, None, :]
                y_t = jnp.einsum('ben,bn->be', state, C_t)
                return (state, y_t)
            xs = (jnp.moveaxis(delta, -1, 0), jnp.moveaxis(Bm, -1, 0), jnp.moveaxis(Cm, -1, 0), jnp.moveaxis(u, -1, 0))
            state0 = jnp.zeros((b, DI, DS), delta.dtype)
            _, ys = jax.lax.scan(step, state0, xs)
            y = jnp.moveaxis(ys, 0, -1)
            y = y + D[None, :, None] * u
            y = y * jax.nn.silu(z)
            return jnp.swapaxes(y, 1, 2)
        key = jax.random.key(seed)
        ks = jax.random.split(key, 8)
        hidden_states = jax.random.normal(ks[0], (B, L, DM), jnp.float32)
        z = jax.random.normal(ks[1], (B, DI, L), jnp.float32)
        in_proj_w = jax.random.normal(ks[2], (DI, DM), jnp.float32) * DM ** (-0.5)
        conv_w = jax.random.normal(ks[3], (DI, DC), jnp.float32) * DC ** (-0.5)
        conv_b = jnp.zeros((DI,), jnp.float32)
        x_proj_w = jax.random.normal(ks[4], (DR + 2 * DS, DI), jnp.float32) * DI ** (-0.5)
        dt_std = DR ** (-0.5)
        dt_proj_w = jax.random.uniform(ks[5], (DI, DR), jnp.float32, -dt_std, dt_std)
        dt = jnp.exp(jax.random.uniform(ks[6], (DI,), jnp.float32) * (math.log(DT_MAX) - math.log(DT_MIN)) + math.log(DT_MIN))
        dt = jnp.clip(dt, DT_FLOOR)
        dt_proj_b = dt + jnp.log(-jnp.expm1(-dt))
        A_log = jnp.log(jnp.broadcast_to(jnp.arange(1, DS + 1, dtype=jnp.float32), (DI, DS)))
        D = jnp.ones((DI,), jnp.float32)
        return dict(hidden_states=hidden_states, z=z, in_proj_w=in_proj_w, conv_w=conv_w, conv_b=conv_b, x_proj_w=x_proj_w, dt_proj_w=dt_proj_w, dt_proj_b=dt_proj_b, A_log=A_log, D=D)
    _L0_xattn_all = _L0_xattn_setup()
    _L0_xattn_in = {k: v for k, v in _L0_xattn_all.items() if k in ('in_proj_w', 'conv_w', 'conv_b', 'x_proj_w', 'dt_proj_w', 'dt_proj_b', 'A_log', 'D')}
    del _L0_xattn_all

    def _L0_ffn_setup():
        import jax, jax.numpy as jnp
        import numpy as np
        HIDDEN = 512
        INTER = 1376
        LUT_SIZE = 16

        def _ghost_linear(x, idx, lut):
            w = lut[idx]
            return jnp.einsum('bsh,oh->bso', x, w)
        key = jax.random.key(seed)
        k_x, k_lut, k_g, k_u, k_d = jax.random.split(key, 5)
        x = jax.random.normal(k_x, (2, 1024, HIDDEN), dtype=jnp.float32)
        lut = jax.random.normal(k_lut, (LUT_SIZE,), dtype=jnp.float32) * 0.02
        gate_idx = jax.random.randint(k_g, (INTER, HIDDEN), 0, LUT_SIZE, dtype=jnp.int32)
        up_idx = jax.random.randint(k_u, (INTER, HIDDEN), 0, LUT_SIZE, dtype=jnp.int32)
        down_idx = jax.random.randint(k_d, (HIDDEN, INTER), 0, LUT_SIZE, dtype=jnp.int32)
        return {'x': x, 'lut': lut, 'gate_idx': gate_idx, 'up_idx': up_idx, 'down_idx': down_idx}
    _L0_ffn_all = _L0_ffn_setup()
    _L0_ffn_in = {k: v for k, v in _L0_ffn_all.items() if k in ('lut', 'gate_idx', 'up_idx', 'down_idx')}
    del _L0_ffn_all
    return {'x': x, 'ctx_1024': ctx_1024, 'L0_attn_weight_qkv': _L0_attn_in['weight_qkv'], 'L0_attn_weight_proj': _L0_attn_in['weight_proj'], 'L0_xattn_in_proj_w': _L0_xattn_in['in_proj_w'], 'L0_xattn_conv_w': _L0_xattn_in['conv_w'], 'L0_xattn_conv_b': _L0_xattn_in['conv_b'], 'L0_xattn_x_proj_w': _L0_xattn_in['x_proj_w'], 'L0_xattn_dt_proj_w': _L0_xattn_in['dt_proj_w'], 'L0_xattn_dt_proj_b': _L0_xattn_in['dt_proj_b'], 'L0_xattn_A_log': _L0_xattn_in['A_log'], 'L0_xattn_D': _L0_xattn_in['D'], 'L0_ffn_lut': _L0_ffn_in['lut'], 'L0_ffn_gate_idx': _L0_ffn_in['gate_idx'], 'L0_ffn_up_idx': _L0_ffn_in['up_idx'], 'L0_ffn_down_idx': _L0_ffn_in['down_idx']}

def reference(x, ctx_1024, L0_attn_weight_qkv, L0_attn_weight_proj, L0_xattn_in_proj_w, L0_xattn_conv_w, L0_xattn_conv_b, L0_xattn_x_proj_w, L0_xattn_dt_proj_w, L0_xattn_dt_proj_b, L0_xattn_A_log, L0_xattn_D, L0_ffn_lut, L0_ffn_gate_idx, L0_ffn_up_idx, L0_ffn_down_idx):
    import jax
    import jax.numpy as jnp

    def _L0_attn_ref(x, weight_qkv, weight_proj):
        import jax, jax.numpy as jnp
        import numpy as np
        HIDDEN = 512
        NUM_HEADS = 16
        NUM_KV_HEADS = 4
        HEAD_DIM = HIDDEN // NUM_HEADS
        Q_PER_KV = NUM_HEADS // NUM_KV_HEADS
        GROUP_SIZE = (Q_PER_KV + 2) * HEAD_DIM
        TOTAL_PROJ = NUM_KV_HEADS * GROUP_SIZE
        SEQ, BATCH = (512, 2)
        seq, batch, hidden = x.shape
        q_size = Q_PER_KV * HEAD_DIM
        qkv = x.reshape(-1, hidden) @ weight_qkv.T
        qkv = qkv.reshape(-1, NUM_KV_HEADS, GROUP_SIZE)
        q = qkv[:, :, :q_size].reshape(seq, batch, NUM_HEADS, HEAD_DIM)
        k = qkv[:, :, q_size:q_size + HEAD_DIM].reshape(seq, batch, NUM_KV_HEADS, HEAD_DIM)
        v = qkv[:, :, q_size + HEAD_DIM:].reshape(seq, batch, NUM_KV_HEADS, HEAD_DIM)
        k = jnp.repeat(k, Q_PER_KV, axis=2)
        v = jnp.repeat(v, Q_PER_KV, axis=2)
        q = q.transpose(1, 2, 0, 3)
        k = k.transpose(1, 2, 0, 3)
        v = v.transpose(1, 2, 0, 3)
        scale = 1.0 / np.sqrt(HEAD_DIM)
        scores = jnp.einsum('bhqd,bhkd->bhqk', q, k) * scale
        causal = jnp.tril(jnp.ones((seq, seq), dtype=bool))
        scores = jnp.where(causal, scores, jnp.float32(-jnp.inf))
        probs = jax.nn.softmax(scores, axis=-1)
        attn = jnp.einsum('bhqk,bhkd->bhqd', probs, v)
        attn = attn.transpose(2, 0, 1, 3).reshape(seq * batch, NUM_HEADS * HEAD_DIM)
        out = attn @ weight_proj.T
        return out.reshape(seq, batch, hidden)

    def _L0_xattn_ref(hidden_states, z, in_proj_w, conv_w, conv_b, x_proj_w, dt_proj_w, dt_proj_b, A_log, D):
        import jax, jax.numpy as jnp
        import numpy as np
        import math
        B, L, DM = (2, 512, 256)
        DS, DC, EXP = (16, 4, 2)
        DI = EXP * DM
        DR = math.ceil(DM / 16)
        DT_MIN, DT_MAX, DT_FLOOR = (0.001, 0.1, 0.0001)

        def _ssm_forward(hidden_states, z, in_proj_w, conv_w, conv_b, x_proj_w, dt_proj_w, dt_proj_b, A_log, D):
            b = hidden_states.shape[0]
            x = jnp.einsum('ed,bld->bel', in_proj_w, hidden_states)
            xp = jnp.pad(x, ((0, 0), (0, 0), (DC - 1, 0)))
            xc = jax.lax.conv_general_dilated(xp, conv_w[:, None, :], window_strides=(1,), padding='VALID', dimension_numbers=('NCH', 'OIH', 'NCH'), feature_group_count=DI)
            u = jax.nn.silu(xc + conv_b[None, :, None])
            x_dbl = jnp.einsum('ke,bel->bkl', x_proj_w, u)
            dt_lo = x_dbl[:, :DR]
            Bm = x_dbl[:, DR:DR + DS]
            Cm = x_dbl[:, DR + DS:]
            delta = jax.nn.softplus(jnp.einsum('er,brl->bel', dt_proj_w, dt_lo) + dt_proj_b[None, :, None])
            A = -jnp.exp(A_log)

            def step(state, xs):
                d_t, B_t, C_t, u_t = xs
                dA = jnp.exp(d_t[..., None] * A)
                state = state * dA + (d_t * u_t)[..., None] * B_t[:, None, :]
                y_t = jnp.einsum('ben,bn->be', state, C_t)
                return (state, y_t)
            xs = (jnp.moveaxis(delta, -1, 0), jnp.moveaxis(Bm, -1, 0), jnp.moveaxis(Cm, -1, 0), jnp.moveaxis(u, -1, 0))
            state0 = jnp.zeros((b, DI, DS), delta.dtype)
            _, ys = jax.lax.scan(step, state0, xs)
            y = jnp.moveaxis(ys, 0, -1)
            y = y + D[None, :, None] * u
            y = y * jax.nn.silu(z)
            return jnp.swapaxes(y, 1, 2)
        return _ssm_forward(hidden_states, z, in_proj_w, conv_w, conv_b, x_proj_w, dt_proj_w, dt_proj_b, A_log, D)

    def _L0_ffn_ref(x, lut, gate_idx, up_idx, down_idx):
        import jax, jax.numpy as jnp
        import numpy as np
        HIDDEN = 512
        INTER = 1376
        LUT_SIZE = 16

        def _ghost_linear(x, idx, lut):
            w = lut[idx]
            return jnp.einsum('bsh,oh->bso', x, w)
        gate = _ghost_linear(x, gate_idx, lut)
        up = _ghost_linear(x, up_idx, lut)
        h = jax.nn.silu(gate) * up
        return _ghost_linear(h, down_idx, lut)
    x = _layernorm(x + _L0_attn_ref(x, L0_attn_weight_qkv, L0_attn_weight_proj), axis=-1)
    x = _layernorm(x + _L0_xattn_ref(ctx_1024, x, L0_xattn_in_proj_w, L0_xattn_conv_w, L0_xattn_conv_b, L0_xattn_x_proj_w, L0_xattn_dt_proj_w, L0_xattn_dt_proj_b, L0_xattn_A_log, L0_xattn_D), axis=-1)
    x = _layernorm(x + _L0_ffn_ref(x, L0_ffn_lut, L0_ffn_gate_idx, L0_ffn_up_idx, L0_ffn_down_idx), axis=-1)
    return x

_drawn_inputs = setup_inputs


def setup_inputs(seed=0):
    import zlib

    import numpy as np

    out = dict(_drawn_inputs(seed))
    spreads = {'L0_xattn_conv_b': (0.0, 0.1), 'L0_xattn_D': (1.0, 0.2)}
    factors = {'L0_xattn_dt_proj_w': 5.311}
    for name, (base, spread) in spreads.items():
        noise = np.random.default_rng([zlib.crc32(name.encode()), seed]).standard_normal(out[name].shape)
        drawn = base * np.exp(spread * noise) if base else spread * noise
        out[name] = jnp.asarray(drawn.astype(out[name].dtype))
    for name, factor in factors.items():
        out[name] = (out[name] * factor).astype(out[name].dtype)
    return out
```

```python
import concourse.bass as bass
from concourse import mybir
from contextlib import ExitStack

S, L, H = 4, 512, 512
QT, HD = 4, 32
DM, DI, DS, DR, TAPS = 256, 512, 16, 16, 4
P = 128
LQ = L // S
ET = DI // P
HT = H // P
NG = 4
NQ = DS // NG
STEPS = NQ * ET
F = 1376
FT = -(-F // P)
FLAST = F - (FT - 1) * P
WCH = 2 * H + H
HALF = WCH // 2
EPS = 1e-5
MASKED = -1e30
PRIMED = 1

def decoder_kernel(nc, xT, x, ctxT, wqkvT, wpT, ipT, chan, xpT, dtT, lut, idx, ident_c, headsum_c, spread_c,
                   pick_c, out):
    f32, bf16, i32 = mybir.dt.float32, mybir.dt.bfloat16, mybir.dt.int32
    ALU, ACT, AX = mybir.AluOpType, mybir.ActivationFunctionType, mybir.AxisListType

    x1_scratch = nc.dram_tensor("x1_scratch", [S, L, H], f32, kind="Internal").ap()
    y_scratch = nc.dram_tensor("y_scratch", [S, DI, L], f32, kind="Internal").ap()
    x2_scratch = nc.dram_tensor("x2_scratch", [S, L, H], f32, kind="Internal").ap()

    top = ExitStack()
    with top:
        def sem(name, ctx=top):
            return ctx.enter_context(nc.semaphore(name))

        ident = top.enter_context(nc.sbuf_tensor("ident", [P, P], f32))
        banks = top.enter_context(nc.psum_tensor("banks", [P, 8, 512], f32))
        stats = top.enter_context(nc.sbuf_tensor("stats", [P, 4, 6], f32))
        meanvar = top.enter_context(nc.sbuf_tensor("meanvar", [P, 4, 2], f32))
        vareps = top.enter_context(nc.sbuf_tensor("vareps", [P, 4], f32))
        rstd = top.enter_context(nc.sbuf_tensor("rstd", [P, 4], f32))
        shift = top.enter_context(nc.sbuf_tensor("shift", [P, 4], f32))
        minus_half = top.enter_context(nc.sbuf_tensor("minus_half", [P, 4], f32))

        stage1(nc, top, ident, banks, (stats, meanvar, vareps, rstd, shift, minus_half), xT, x, ctxT, wqkvT, wpT,
               ipT, chan, xpT, dtT, ident_c, headsum_c, spread_c, pick_c, x1_scratch, y_scratch)
        stage234(nc, top, ident, banks, (stats, meanvar, vareps, rstd, shift, minus_half), lut, idx,
                 x1_scratch, y_scratch, x2_scratch, out)


def stage1(nc, top, ident, banks, ln, xT, x, ctxT, wqkvT, wpT, ipT, chan, xpT, dtT, ident_c, headsum_c,
           spread_c, pick_c, x1_scratch, y_scratch):
    f32, bf16 = mybir.dt.float32, mybir.dt.bfloat16
    ALU, ACT, AX = mybir.AluOpType, mybir.ActivationFunctionType, mybir.AxisListType
    stats, meanvar, vareps, rstd, shift, minus_half = ln
    ctx = ExitStack()
    with ctx:
        def sb(name, shape, dt=f32):
            return ctx.enter_context(nc.sbuf_tensor(name, shape, dt))

        def sem(name):
            return ctx.enter_context(nc.semaphore(name))

        wqkv = sb("wqkv", [P, HT, 6 * P])
        wp = sb("wp", [P, QT, H])
        ip = sb("ip", [P, DM // P, DI])
        ch = sb("ch", [P, ET, TAPS + 3 + DS])
        xp_w = sb("xp_w", [P, ET, 3 * DS])
        dt_w = sb("dt_w", [DR, DI])
        headsum = sb("headsum", [P, QT, 32])
        spread = sb("spread", [P, S * QT, P])
        pick = sb("pick", [96, 32], bf16)
        negA = sb("negA", [P, ET, DS])
        ctx_sb = sb("ctx_sb", [P, DM // P, L])
        xT_sb = sb("xT_sb", [P, HT, S, LQ])
        x_sb = sb("x_sb", [P, S, H])
        q = sb("q", [P, QT, S, LQ])
        kv = sb("kv", [P, 2, S, LQ])
        prod = sb("prod", [P, 2, QT, S, LQ])
        prob = sb("prob", [P, S, LQ])
        rowmax = sb("rowmax", [P, LQ])
        rowsum = sb("rowsum", [P, LQ])
        rowinv = sb("rowinv", [P, LQ])
        conv_in = sb("conv_in", [P, ET, TAPS - 1 + L])
        u = sb("u", [P, ET, L])
        bc_parts = sb("bc_parts", [96, L], bf16)
        bc_rest = sb("bc_rest", [32, L])
        bc_mid = sb("bc_mid", [32, L], bf16)
        dt_lo = sb("dt_lo", [DR, L])
        delta = sb("delta", [P, ET, L])
        du = sb("du", [P, ET, L])
        brep = sb("brep", [P, 2, NG, L])
        crep = sb("crep", [P, 2, NG, L])
        decay = sb("decay", [P, 2, NG, L])
        state = sb("state", [P, 3, NG, L])
        y_sb = sb("y_sb", [P, ET, L])
        conv_w = lambda et, j: ch[:, et, j:j + 1]
        conv_b = lambda et: ch[:, et, TAPS:TAPS + 1]
        dt_b = lambda et: ch[:, et, TAPS + 1:TAPS + 2]
        skip_d = lambda et: ch[:, et, TAPS + 2:TAPS + 3]
        a_log = ch[:, :, TAPS + 3:TAPS + 3 + DS]
        k, v = kv[:, 0], kv[:, 1]
        conv_acc, expneg, relu = state[:, 0], state[:, 1], state[:, 2]

        (ip_in, w_in, ctx_in, xT_in, x_in, negA_ready, setup_done, inproj_out, qkv_out, bc_out, dt_out,
         delta_out, score_out, rep_out, pb_out, proj_out, nsum_done, xp_ready, qkv_ready, conv_tap, u_ready,
         bc_hi, bc_r1, bc_m, bc_lo, dtlo_ready, abs_ready, expneg_ready, onep_ready, ln_ready, corr_ready,
         base_ready, relu_ready, delta_ready, du_ready, prod_ready, masked, max_ready, sub_ready, exp_ready,
         sum_ready, inv_ready, prob_ready, pv_mul, pv_sum, rep_ready, decay_ready, dbu_ready, scan_ready,
         hc_ready, res_ready, stat_ready, mv_ready, ve_ready, rstd_ready, shift_ready, x1_ready, x1_out,
         y_ready, y_out, half_ready) = [sem(n) for n in (
             "ip_in w_in ctx_in xT_in x_in negA_ready setup_done inproj_out qkv_out bc_out dt_out "
             "delta_out score_out rep_out pb_out proj_out nsum_done xp_ready qkv_ready conv_tap u_ready "
             "bc_hi bc_r1 bc_m bc_lo dtlo_ready abs_ready expneg_ready onep_ready ln_ready corr_ready "
             "base_ready relu_ready delta_ready du_ready prod_ready masked max_ready sub_ready exp_ready "
             "sum_ready inv_ready prob_ready pv_mul pv_sum rep_ready decay_ready dbu_ready scan_ready "
             "hc_ready res_ready stat_ready mv_ready ve_ready rstd_ready shift_ready x1_ready x1_out "
             "y_ready y_out half_ready").split()]
        N_W = 8

        with nc.Block() as block:

            @block.sync
            def _(sp):
                sp.dma_start(ip[:], ipT.rearrange("(t p) n -> p t n", p=P)).then_inc(ip_in, 16)
                sp.dma_start(ch[:], chan).then_inc(ip_in, 16)

                def load(b, first=False):
                    if not first:
                        sp.wait_ge(inproj_out, b * ET)
                    sp.dma_start(ctx_sb[:], ctxT.rearrange("(t p) (b l) -> p t b l", p=P, b=S)[:, :, b, :])\
                        .then_inc(ctx_in, 16)
                    if not first:
                        sp.wait_ge(qkv_out, b * 6)
                    for t in range(HT):
                        sp.dma_start(xT_sb[:, t], xT.rearrange("(t p) (s c l) -> t p s c l", p=P, s=S, c=S)[t, :, :, b, :])\
                            .then_inc(xT_in, 16)
                    if not first:
                        sp.wait_ge(x1_out, b * 16)
                    sp.dma_start(x_sb[:], x.rearrange("s (c p) h -> p s c h", p=P)[:, :, b, :]).then_inc(x_in, 16)

                load(0, first=True)
                with sp.Fori(1, S) as b:
                    load(b)

            @block.tensor
            def _(pe):
                mm = nc.tensor.matmul
                pe.sem_inc(nsum_done, PRIMED)
                pe.wait_ge(ip_in, 32)
                with pe.Fori(0, S) as b:
                    pe.wait_ge(ctx_in, b * 16 + 16)
                    pe.wait_ge(res_ready, PRIMED + b * S)
                    pe.wait_ge(rep_ready, PRIMED + b * 2 * DS)
                    for et in range(ET):
                        for t in range(DM // P):
                            last = mm(banks[:, et, :], ip[:, t, et * P:(et + 1) * P], ctx_sb[:, t, :],
                                      start=t == 0, stop=t == DM // P - 1)
                        last.then_inc(inproj_out, 1)
                    pe.wait_ge(w_in, N_W * 16)
                    pe.wait_ge(xT_in, b * 64 + 64)
                    for m in range(6):
                        if m < 4:
                            pe.wait_ge(xp_ready, b * ET + m + 1)
                        else:
                            pe.wait_ge(qkv_ready, b * 6 + m - 3)
                        for t in range(HT):
                            last = mm(banks[:, m % 4, :], wqkv[:, t, m * P:(m + 1) * P],
                                      xT_sb[:, t].rearrange("p s l -> p (s l)"), start=t == 0, stop=t == HT - 1)
                        last.then_inc(qkv_out, 1)
                    pe.wait_ge(u_ready, b * ET + ET)
                    pe.wait_ge(qkv_ready, b * 6 + 3)
                    for et in range(ET):
                        last = mm(banks[0:2 * DS, 2, :], xp_w[:, et, 0:2 * DS], u[:, et, :],
                                  start=et == 0, stop=et == ET - 1)
                    last.then_inc(bc_out, 1)
                    pe.wait_ge(qkv_ready, b * 6 + 4)
                    for et in range(ET):
                        last = mm(banks[0:DR, 3, :], xp_w[:, et, 2 * DS:3 * DS], u[:, et, :],
                                  start=et == 0, stop=et == ET - 1)
                    last.then_inc(dt_out, 1)
                    pe.wait_ge(dtlo_ready, b + 1)
                    pe.wait_ge(qkv_ready, b * 6 + 6)
                    pe.wait_ge(bc_r1, b + 1)
                    for et in range(ET):
                        mm(banks[:, et, :], dt_w[:, et * P:(et + 1) * P], dt_lo[:],
                           start=True, stop=True).then_inc(delta_out, 1)
                    pe.wait_ge(relu_ready, b * ET + 1)
                    for i in range(S):
                        pe.wait_ge(prod_ready, b * S + i + 1)
                        for qt in range(QT):
                            last = mm(banks[32 * i:32 * i + 32, 0, 0:(i + 1) * LQ], headsum[:, qt, :],
                                      prod[:, i % 2, qt, 0:i + 1, :].rearrange("p j l -> p (j l)"),
                                      start=qt == 0, stop=qt == QT - 1)
                        last.then_inc(score_out, 1)

                    def repeat_rows(g):
                        for r in range(2 * NG):
                            if r < 2 and g == 0:
                                pe.wait_ge(relu_ready, b * ET + 3 + r)
                            else:
                                pe.wait_ge(rep_ready, PRIMED + b * 2 * DS + 2 * NG * g + r - 1)
                            row = (DS if r >= NG else 0) + NG * g + r % NG
                            mm(banks[:, 2 + r % 2, :], pick[:, row:row + 1].to_broadcast([96, P]), bc_parts[:],
                               start=True, stop=True).then_inc(rep_out, 1)

                    pe.wait_ge(bc_lo, b + 1)
                    pe.wait_ge(bc_m, b * 2 + 2)
                    repeat_rows(0)
                    pe.wait_ge(prob_ready, b + 1)
                    pe.wait_ge(y_ready, PRIMED + b * ET)
                    for i in range(S):
                        for h in range(2):
                            if i:
                                pe.wait_ge(pv_mul, b * 8 + 2 * (i - 1) + h + 1)
                            for c in range(2):
                                last = mm(banks[:, 4 + 2 * h + c, 0:(i + 1) * LQ], spread[:, i * QT + 2 * h + c, :],
                                          prob[:, 0:i + 1, :].rearrange("p j l -> p (j l)"), start=True, stop=True)
                            last.then_inc(pb_out, 1)
                    pe.wait_ge(pv_sum, PRIMED + b * 8 + 8)
                    for s in range(S):
                        if s == 0:
                            pe.wait_ge(sub_ready, b + 1)
                        elif s >= 2:
                            pe.wait_ge(res_ready, PRIMED + b * S + s - 1)
                        for qt in range(QT):
                            last = mm(banks[:, s % 2, :], q[:, qt, s, :], wp[:, qt, :],
                                      start=qt == 0, stop=qt == QT - 1)
                        last.then_inc(proj_out, 1)
                    for t in range(STEPS):
                        g, et = t // ET, t % ET
                        pe.wait_ge(hc_ready, PRIMED + b * STEPS + t + 1)
                        for n in range(NG):
                            last = mm(banks[:, 4 + et, :], ident[:], state[:, t % 3, n, :],
                                      start=(g == 0 and n == 0), stop=(g == NQ - 1 and n == NG - 1))
                        last.then_inc(nsum_done, 1)
                        if et == 0 and g < NQ - 1:
                            repeat_rows(g + 1)

            @block.scalar
            def _(act):
                A = nc.scalar.activation
                act.dma_start(wqkv[:], wqkvT.rearrange("(t p) n -> p t n", p=P)).then_inc(w_in, 16)
                act.dma_start(xp_w[:], xpT.rearrange("(t p) n -> p t n", p=P)).then_inc(w_in, 16)
                act.dma_start(dt_w[:], dtT).then_inc(w_in, 16)
                act.dma_start(pick[:], pick_c).then_inc(w_in, 16)
                act.dma_start(headsum[:], headsum_c).then_inc(w_in, 16)
                act.dma_start(spread[:], spread_c).then_inc(w_in, 16)
                act.dma_start(wp[:], wpT.rearrange("(t p) n -> p t n", p=P)).then_inc(w_in, 16)
                act.dma_start(ident[:], ident_c).then_inc(w_in, 16)
                act.wait_ge(ip_in, 32)
                A(negA[:], a_log, ACT.Exp).then_inc(negA_ready, 1)
                act.sem_inc(rep_ready, PRIMED)
                act.wait_ge(setup_done, 4)
                with act.Fori(0, S) as b:
                    act.wait_ge(conv_tap, PRIMED + b * 16)
                    for et in range(ET):
                        act.wait_ge(inproj_out, b * ET + et + 1)
                        A(conv_in[:, et, TAPS - 1:], banks[:, et, :], ACT.Copy).then_inc(xp_ready, 1)
                    act.wait_ge(pv_sum, PRIMED + b * 8)
                    act.wait_ge(res_ready, PRIMED + b * S)
                    for m in range(6):
                        act.wait_ge(qkv_out, b * 6 + m + 1)
                        dst = q[:, m] if m < QT else kv[:, m - QT]
                        A(dst.rearrange("p s l -> p (s l)"), banks[:, m % 4, :], ACT.Copy).then_inc(qkv_ready, 1)
                    act.wait_ge(y_ready, PRIMED + b * ET)
                    for et in range(ET):
                        act.wait_ge(conv_tap, PRIMED + b * 16 + 12 + et + 1)
                        A(u[:, et, :], conv_acc[:, et, :], ACT.Silu).then_inc(u_ready, 1)
                    act.wait_ge(bc_out, b + 1)
                    A(bc_parts[0:32, :], banks[0:32, 2, :], ACT.Copy).then_inc(bc_hi, 1)
                    act.wait_ge(dt_out, b + 1)
                    A(dt_lo[:], banks[0:DR, 3, :], ACT.Copy).then_inc(dtlo_ready, 1)
                    act.wait_ge(bc_r1, b + 1)
                    A(bc_mid[:], bc_rest[:], ACT.Copy).then_inc(bc_m, 1)
                    A(bc_parts[32:64, :], bc_rest[:], ACT.Copy).then_inc(bc_m, 1)
                    act.wait_ge(nsum_done, PRIMED + b * STEPS)
                    for et in range(ET):
                        act.wait_ge(delta_out, b * ET + et + 1)
                        A(expneg[:, et, :], banks[:, et, :], ACT.Abs, bias=dt_b(et)).then_inc(abs_ready, 1)
                    act.wait_ge(abs_ready, b * ET + ET)
                    A(expneg[:], expneg[:], ACT.Exp, scale=-1.0).then_inc(expneg_ready, 1)
                    act.wait_ge(onep_ready, b + 1)
                    A(delta[:], conv_acc[:], ACT.Ln).then_inc(ln_ready, 1)
                    act.wait_ge(sub_ready, b + 1)
                    A(prob[:], prob[:], ACT.Exp, scale=float(HD) ** -0.5).then_inc(exp_ready, 1)

                    def keep_rows(g, rs):
                        for r in rs:
                            act.wait_ge(rep_out, b * 2 * DS + 2 * NG * g + r + 1)
                            dst = brep if r < NG else crep
                            A(dst[:, g % 2, r % NG, :], banks[:, 2 + r % 2, :], ACT.Copy).then_inc(rep_ready, 1)

                    act.wait_ge(dbu_ready, PRIMED + b * STEPS)
                    act.wait_ge(hc_ready, PRIMED + b * STEPS)
                    keep_rows(0, range(2 * NG))
                    act.wait_ge(delta_ready, b + 1)
                    for t in range(STEPS):
                        g, et = t // ET, t % ET
                        act.wait_ge(scan_ready, PRIMED + b * STEPS + max(t - 1, 0))
                        for n in range(NG):
                            A(decay[:, t % 2, n, 1:], delta[:, et, 1:], ACT.Exp,
                              scale=negA[:, et, NG * g + n:NG * g + n + 1]).then_inc(decay_ready, 1)
                        if g < NQ - 1 and et in (1, 2):
                            if g and et == 1:
                                act.wait_ge(hc_ready, PRIMED + b * STEPS + ET * g)
                            keep_rows(g + 1, range(NG * (et - 1), NG * et))
                        if t == 6:
                            act.wait_ge(shift_ready, b + 1)
                            for s in range(S):
                                A(x_sb[:, s, :], x_sb[:, s, :], ACT.Identity, bias=shift[:, s:s + 1],
                                  scale=rstd[:, s:s + 1]).then_inc(x1_ready, 1)

            @block.vector
            def _(dve):
                V = nc.vector
                V.memset(decay[:, :, :, 0:1], 0.0).then_inc(setup_done, 1)
                V.memset(conv_in[:, :, 0:TAPS - 1], 0.0).then_inc(setup_done, 1)
                V.memset(prob[:], 0.0).then_inc(setup_done, 1)
                dve.wait_ge(negA_ready, 1)
                V.tensor_scalar(negA[:], negA[:], -1.0, None, ALU.mult).then_inc(setup_done, 1)
                for primed in (res_ready, y_ready, conv_tap, pv_sum, dbu_ready, scan_ready):
                    dve.sem_inc(primed, PRIMED)
                with dve.Fori(0, S) as b:
                    dve.wait_ge(nsum_done, PRIMED + b * STEPS)
                    for j in range(TAPS):
                        for et in range(ET):
                            tap = conv_in[:, et, j:j + L]
                            if j == 0:
                                dve.wait_ge(xp_ready, b * ET + et + 1)
                                V.tensor_scalar(conv_acc[:, et, :], tap, conv_w(et, 0), conv_b(et), ALU.mult,
                                                ALU.add).then_inc(conv_tap, 1)
                            else:
                                dve.wait_ge(conv_tap, PRIMED + b * 16 + 4 * (j - 1) + et + 1)
                                V.scalar_tensor_tensor(conv_acc[:, et, :], tap, conv_w(et, j), conv_acc[:, et, :],
                                                       ALU.mult, ALU.add).then_inc(conv_tap, 1)
                    def score_product(i):
                        if i >= 2:
                            dve.wait_ge(score_out, b * S + i - 1)
                        shape = [P, QT, i + 1, LQ]
                        V.tensor_tensor(prod[:, i % 2, :, 0:i + 1, :], q[:, :, i:i + 1, :].to_broadcast(shape),
                                        k[:, 0:i + 1, :].unsqueeze(1).to_broadcast(shape), ALU.mult)\
                            .then_inc(prod_ready, 1)

                    dve.wait_ge(qkv_ready, b * 6 + 5)
                    score_product(0)
                    score_product(1)
                    dve.wait_ge(bc_hi, b + 1)
                    V.tensor_tensor(bc_rest[:], banks[0:32, 2, :], bc_parts[0:32, :], ALU.subtract).then_inc(bc_r1, 1)
                    dve.wait_ge(bc_r1, b + 1)
                    dve.wait_ge(bc_m, b * 2 + 1)
                    V.tensor_tensor(bc_parts[64:96, :], bc_rest[:], bc_mid[:], ALU.subtract).then_inc(bc_lo, 1)
                    for et in range(ET):
                        dve.wait_ge(abs_ready, b * ET + et + 1)
                        V.tensor_scalar(relu[:, et, :], banks[:, et, :], dt_b(et), 0.0, ALU.add, ALU.max)\
                            .then_inc(relu_ready, 1)
                    score_product(2)
                    score_product(3)
                    dve.wait_ge(expneg_ready, b + 1)
                    V.tensor_scalar(conv_acc[:], expneg[:], 1.0, None, ALU.add).then_inc(onep_ready, 1)
                    dve.wait_ge(onep_ready, b + 1)
                    V.scalar_tensor_tensor(expneg[:], conv_acc[:], -1.0, expneg[:], ALU.add, ALU.subtract)\
                        .then_inc(corr_ready, 1)
                    dve.wait_ge(corr_ready, b + 1)
                    dve.wait_ge(relu_ready, b * ET + ET)
                    V.tensor_tensor(relu[:], relu[:], expneg[:], ALU.subtract).then_inc(base_ready, 1)
                    dve.wait_ge(base_ready, b + 1)
                    dve.wait_ge(ln_ready, b + 1)
                    V.tensor_tensor(delta[:], delta[:], relu[:], ALU.add).then_inc(delta_ready, 1)
                    dve.wait_ge(score_out, b * S + S)
                    for i in range(S - 1):
                        V.memset(banks[32 * i:32 * i + 32, 0, (i + 1) * LQ:], MASKED).then_inc(masked, 1)
                    dve.wait_ge(masked, b * 3 + 3)
                    sc = banks[:, 0, :].rearrange("p (j l) -> p j l", j=S)
                    V.tensor_reduce(rowmax[:], sc.rearrange("p j l -> p l j"), AX.X, ALU.max).then_inc(max_ready, 1)
                    dve.wait_ge(max_ready, b + 1)
                    V.tensor_tensor(prob[:], sc, rowmax[:].unsqueeze(1).to_broadcast([P, S, LQ]), ALU.subtract)\
                        .then_inc(sub_ready, 1)
                    dve.wait_ge(exp_ready, b + 1)
                    V.tensor_reduce(rowsum[:], prob[:].rearrange("p j l -> p l j"), AX.X, ALU.add)\
                        .then_inc(sum_ready, 1)
                    dve.wait_ge(sum_ready, b + 1)
                    V.reciprocal(rowinv[:], rowsum[:]).then_inc(inv_ready, 1)
                    dve.wait_ge(inv_ready, b + 1)
                    V.tensor_tensor(prob[:], prob[:], rowinv[:].unsqueeze(1).to_broadcast([P, S, LQ]), ALU.mult)\
                        .then_inc(prob_ready, 1)

                    dve.wait_ge(qkv_ready, b * 6 + 6)

                    def pv_product(i, h):
                        dve.wait_ge(pb_out, b * 8 + 2 * i + h + 1)
                        if i:
                            dve.wait_ge(pv_sum, PRIMED + b * 8 + 2 * (i - 1) + h + 1)
                        shape = [P, 2, i + 1, LQ]
                        pb = banks[:, 4 + 2 * h:6 + 2 * h, 0:(i + 1) * LQ].rearrange("p c (j l) -> p c j l", l=LQ)
                        V.tensor_tensor(prod[:, h, 0:2, 0:i + 1, :], pb,
                                        v[:, 0:i + 1, :].unsqueeze(1).to_broadcast(shape), ALU.mult)\
                            .then_inc(pv_mul, 1)

                    def pv_total(i, h):
                        dve.wait_ge(pv_mul, b * 8 + 2 * i + h + 1)
                        V.tensor_reduce(q[:, 2 * h:2 * h + 2, i, :],
                                        prod[:, h, 0:2, 0:i + 1, :].rearrange("p c j l -> p c l j"), AX.X, ALU.add)\
                            .then_inc(pv_sum, 1)

                    pv_product(0, 0)
                    pv_product(0, 1)
                    for i in range(S):
                        pv_total(i, 0)
                        pv_total(i, 1)
                        if i < S - 1:
                            pv_product(i + 1, 0)
                            pv_product(i + 1, 1)

                    def input_product(t):
                        g, et = t // ET, t % ET
                        if t >= 3:
                            dve.wait_ge(nsum_done, PRIMED + b * STEPS + t - 2)
                        dve.wait_ge(rep_ready, PRIMED + b * 2 * DS + 2 * NG * g + NG)
                        dve.wait_ge(du_ready, b * ET + min(t, ET - 1) + 1)
                        V.tensor_tensor(state[:, t % 3], du[:, et:et + 1, :].to_broadcast([P, NG, L]),
                                        brep[:, g % 2], ALU.mult).then_inc(dbu_ready, 1)

                    def scan(t):
                        dve.wait_ge(dbu_ready, PRIMED + b * STEPS + t + 1)
                        dve.wait_ge(decay_ready, b * STEPS * NG + NG * t + NG)
                        flat = state[:, t % 3].rearrange("p n l -> p (n l)")
                        V.tensor_tensor_scan(flat, decay[:, t % 2].rearrange("p n l -> p (n l)"), flat, 0.0,
                                             ALU.mult, ALU.add).then_inc(scan_ready, 1)

                    input_product(0)
                    for t in range(STEPS):
                        if t + 1 < STEPS:
                            input_product(t + 1)
                        scan(t)
                        if t < S:
                            dve.wait_ge(proj_out, b * S + t + 1)
                            if t == 0:
                                dve.wait_ge(x_in, b * 16 + 16)
                            V.tensor_tensor(x_sb[:, t, :], banks[:, t % 2, :], x_sb[:, t, :], ALU.add)\
                                .then_inc(res_ready, 1)
                            dve.wait_ge(res_ready, PRIMED + b * S + t + 1)
                            V.bn_stats(stats[:, t, :], x_sb[:, t, :]).then_inc(stat_ready, 1)
                            dve.wait_ge(setup_done, 4)
                            dve.wait_ge(stat_ready, b * S + t + 1)
                            V.bn_aggr(meanvar[:, t, :], stats[:, t, :]).then_inc(mv_ready, 1)
                        if t == S:
                            dve.wait_ge(mv_ready, b * S + S)
                            V.tensor_scalar(vareps[:], meanvar[:, :, 1], EPS, None, ALU.add).then_inc(ve_ready, 1)
                        if t == S + 1:
                            dve.wait_ge(rstd_ready, b + 1)
                            V.scalar_tensor_tensor(shift[:], meanvar[:, :, 0], -1.0, rstd[:], ALU.mult, ALU.mult)\
                                .then_inc(shift_ready, 1)
                    for et in range(ET):
                        dve.wait_ge(nsum_done, PRIMED + b * STEPS + STEPS - ET + et + 1)
                        V.scalar_tensor_tensor(y_sb[:, et, :], u[:, et, :], skip_d(et), banks[:, 4 + et, :],
                                               ALU.mult, ALU.add).then_inc(y_ready, 1)

            @block.gpsimd
            def _(pool):
                G = nc.gpsimd
                G.memset(minus_half[:], -0.5).then_inc(half_ready, 1)
                pool.wait_ge(half_ready, 1)
                pool.sem_inc(hc_ready, PRIMED)
                with pool.Fori(0, S) as b:
                    pool.wait_ge(delta_ready, b + 1)
                    for et in range(ET):
                        G.tensor_tensor(du[:, et, :], delta[:, et, :], u[:, et, :], ALU.mult).then_inc(du_ready, 1)
                    for t in range(STEPS):
                        g = t // ET
                        pool.wait_ge(rep_ready, PRIMED + b * 2 * DS + 2 * NG * (g + 1))
                        pool.wait_ge(scan_ready, PRIMED + b * STEPS + t + 1)
                        G.tensor_tensor(state[:, t % 3], state[:, t % 3], crep[:, g % 2], ALU.mult)\
                            .then_inc(hc_ready, 1)
                        if t == S:
                            pool.wait_ge(ve_ready, b + 1)
                            G.tensor_tensor(rstd[:], vareps[:], minus_half[:], ALU.pow).then_inc(rstd_ready, 1)
                        if t == 8:
                            pool.wait_ge(x1_ready, b * S + S)
                            pool.dma_start(x1_scratch.rearrange("s (c p) h -> p s c h", p=P)[:, :, b, :], x_sb[:])\
                                .then_inc(x1_out, 16)
                    pool.wait_ge(y_ready, PRIMED + b * ET + ET)
                    pool.dma_start(y_scratch.rearrange("b (t p) l -> p b t l", p=P)[:, b], y_sb[:])\
                        .then_inc(y_out, 16)
                    pool.wait_ge(y_out, b * 16 + 16)
                pool.wait_ge(x1_out, 16 * S)


def stage234(nc, top, ident, banks, ln, lut, idx, x1_scratch, y_scratch, x2_scratch, out):
    f32, i32 = mybir.dt.float32, mybir.dt.int32
    ALU, ACT, AX = mybir.AluOpType, mybir.ActivationFunctionType, mybir.AxisListType
    stats, meanvar, vareps, rstd, shift, minus_half = ln
    ctx = ExitStack()
    with ctx:
        def sb(name, shape, dt=f32):
            return ctx.enter_context(nc.sbuf_tensor(name, shape, dt))

        def sem(name):
            return ctx.enter_context(nc.semaphore(name))

        table = sb("table", [P, 16])
        table_gap = sb("table_gap", [P, 8])
        x2T = sb("x2T", [P, HT, S * L])
        hT = sb("hT", [P, FT, S * L])
        wd = sb("wd", [P, FT, H])
        wbuf = sb("wbuf", [P, 2, WCH])
        leaf = sb("leaf", [P, 4, HALF])
        bits = sb("bits", [P, 4, HALF], i32)
        idx_sb = sb("idx_sb", [P, 2, WCH], i32)
        silu = sb("silu", [P, 2, 512])
        wait_here = sb("wait_here", [P, 1])
        res = sb("res", [P, 3, H])
        flat_h = hT[:].rearrange("p f n -> p (f n)")
        x1b = [flat_h[:, b * 2048:(b + 1) * 2048].rearrange("p (t h) -> p t h", h=H) for b in range(S)]
        yb = [flat_h[:, (4 + b) * 2048:(5 + b) * 2048].rearrange("p (t h) -> p t h", h=L) for b in range(S)]
        gate = [flat_h[:, (8 + b) * 2048:(9 + b) * 2048].rearrange("p (t h) -> p t h", h=H) for b in range(2)]

        (x1_in, y_in, gate_ready, gated, yT_out, sum_ready, stat_ready, mv_ready, ve_ready, rstd_ready,
         shift_ready, x2_ready, x2_out, x2T_out, x2T_act, x2T_dve, lut_in, gap_ready, idx_in, bits_ready,
         leaf_ready, mux_ready, wd_ready, gate_up_out, silu_ready, h_ready, down_out, x2_in, res_ready,
         stat4_ready, mv4_ready, ve4_ready, rstd4_ready, shift4_ready, out_ready, stored) = [sem(n) for n in (
             "x1_in y_in gate_ready gated yT_out sum2_ready stat2_ready mv2_ready ve2_ready rstd2_ready "
             "shift2_ready x2_ready x2_out x2T_out x2T_act x2T_dve lut_in gap_ready idx_in bits_ready "
             "leaf_ready mux_ready wd_ready gate_up_out silu_ready h_ready down_out x2_in res4_ready "
             "stat4_ready mv4_ready ve4_ready rstd4_ready shift4_ready out_ready stored").split()]
        TT = S * L // P
        TB = S * L // 512
        RR = 3

        LEAF_BUF = [0, 1, 2, 3, 1, 3, 2, 4]
        LEAF_AFTER = [None, 0, 0, 0, 1, 2, 3, 0]
        MUX = [(0, 1, 1), (2, 3, 1), (0, 2, 2), (1, 3, 1), (2, 4, 1), (1, 2, 2), (0, 1, 3)]
        MUX_LEAVES = [2, 4, 4, 6, 8, 8, 8]

        with nc.Block() as block:

            @block.sync
            def _(sp):
                sp.dma_start(table[:], lut.to_broadcast([P, 16])).then_inc(lut_in, 16)
                for b in range(S):
                    sp.dma_start(x1b[b], x1_scratch[b].rearrange("(t p) h -> p t h", p=P)).then_inc(x1_in, 16)
                    sp.wait_ge(x1_in, 16 * b + 16)
                    sp.dma_start(yb[b], y_scratch[b].rearrange("(t p) l -> p t l", p=P)).then_inc(y_in, 16)
                    sp.wait_ge(y_in, 16 * b + 16)
                for f in range(2):
                    sp.dma_start(idx_sb[:, f], idx[f]).then_inc(idx_in, 16)
                    sp.wait_ge(idx_in, 16 * f + 16)
                for b in range(S):
                    sp.wait_ge(x2_ready, b * 4 + 4)
                    sp.dma_start(x2_scratch[b].rearrange("(t p) h -> p t h", p=P), x1b[b]).then_inc(x2_out, 16)
                with sp.Fori(2, FT - 1, 2) as f2:
                    for d in range(2):
                        sp.wait_ge(idx_in, (f2 + d) * 16)
                        sp.wait_ge(bits_ready, (f2 + d) * 8 - 8)
                        sp.dma_start(idx_sb[:, d], idx[f2 + d]).then_inc(idx_in, 16)
                sp.wait_ge(idx_in, (FT - 1) * 16)
                sp.wait_ge(bits_ready, (FT - 1) * 8 - 8)
                sp.dma_start(idx_sb[:, (FT - 1) % 2], idx[FT - 1]).then_inc(idx_in, 16)
                sp.wait_ge(x2_out, 16 * S)
                for t in range(TT + 2):
                    if t < TT:
                        if t >= RR:
                            sp.wait_ge(stored, (t - RR) * 16 + 16)
                        b, c = divmod(t, 4)
                        sp.dma_start(res[:, t % RR, :], x2_scratch[b, c * P:(c + 1) * P, :]).then_inc(x2_in, 16)
                        sp.wait_ge(x2_in, 16 * t + 16)
                    if t >= 2:
                        b, c = divmod(t - 2, 4)
                        sp.wait_ge(out_ready, t - 1)
                        sp.dma_start(out[b, c * P:(c + 1) * P, :], res[:, (t - 2) % RR, :]).then_inc(stored, 16)
                sp.wait_ge(stored, TT * 16)

            @block.tensor
            def _(pe):
                mm = nc.tensor.matmul

                def gated_back(b):
                    pe.wait_ge(gated, b + 1)
                    for lt in range(4):
                        if b:
                            pe.wait_ge(sum_ready, (b - 1) * 4 + lt + 1)
                        for et in range(4):
                            last = nc.tensor.transpose(banks[:, lt, et * P:(et + 1) * P],
                                                       yb[b][:, et, lt * P:(lt + 1) * P], ident[:])
                        last.then_inc(yT_out, 1)

                def x2_over(b):
                    pe.wait_ge(x2_ready, b * 4 + 4)
                    for ht in range(4):
                        if b:
                            pe.wait_ge(x2T_act if ht < 2 else x2T_dve, (b - 1) * 2 + ht % 2 + 1)
                        for lt in range(4):
                            last = nc.tensor.transpose(banks[:, 4 + ht, lt * P:(lt + 1) * P],
                                                       x1b[b][:, lt, ht * P:(ht + 1) * P], ident[:])
                        last.then_inc(x2T_out, 1)

                gated_back(0)
                for b in range(S):
                    if b + 1 < S:
                        gated_back(b + 1)
                    x2_over(b)

                def gate_up(f, par, first):
                    pe.wait_ge(mux_ready, f * 14 + 14)
                    for tb in range(TB):
                        if first:
                            pe.wait_ge(sum_ready, 16)
                            pe.wait_ge(x2T_act, 8)
                            pe.wait_ge(x2T_dve, 8)
                        else:
                            pe.wait_ge(h_ready, f * 4 - 3 + tb)
                        for w in range(2):
                            for t in range(HT):
                                last = mm(banks[:, 2 * tb + w, :], wbuf[:, par, w * H + t * P:w * H + (t + 1) * P],
                                          x2T[:, t, tb * 512:(tb + 1) * 512], start=t == 0, stop=t == HT - 1)
                        last.then_inc(gate_up_out, 1)

                gate_up(0, 0, True)
                with pe.Fori(1, FT - 1, 2) as f:
                    gate_up(f, 1, False)
                    gate_up(f + 1, 0, False)
                pe.wait_ge(wd_ready, FT)
                for t in range(TT):
                    if t < 8:
                        pe.wait_ge(h_ready, FT * 4)
                    else:
                        pe.wait_ge(res_ready, t - 7)
                    for f in range(FT):
                        rows = P if f < FT - 1 else FLAST
                        last = mm(banks[:, t % 8, :], hT[0:rows, f, t * P:(t + 1) * P], wd[0:rows, f, :],
                                  start=f == 0, stop=f == FT - 1)
                    last.then_inc(down_out, 1)

            @block.scalar
            def _(act):
                A = nc.scalar.activation

                def gates(b):
                    act.wait_ge(x1_in, 16 * b + 16)
                    if b >= 2:
                        act.wait_ge(gated, b - 1)
                    A(gate[b % 2], x1b[b], ACT.Silu).then_inc(gate_ready, 1)

                def norm_apply(b):
                    act.wait_ge(shift_ready, b + 1)
                    for lt in range(4):
                        A(x1b[b][:, lt, :], x1b[b][:, lt, :], ACT.Identity, bias=shift[:, lt:lt + 1],
                          scale=rstd[:, lt:lt + 1]).then_inc(x2_ready, 1)

                def keep_x2T(b):
                    for ht in range(2):
                        act.wait_ge(x2T_out, b * 4 + ht + 1)
                        A(x2T[:, ht, b * 512:(b + 1) * 512], banks[:, 4 + ht, :], ACT.Copy).then_inc(x2T_act, 1)

                gates(0)
                gates(1)
                for b in range(S):
                    norm_apply(b)
                    if b + 2 < S:
                        gates(b + 2)
                    keep_x2T(b)

                def leaves(f, par, first=False):
                    for c in range(2):
                        act.wait_ge(bits_ready, f * 8 + 4 * c + 1)
                        for j in range(8):
                            if j == 0:
                                if not first:
                                    act.wait_ge(gate_up_out, f * 4 - 4)
                                    act.wait_ge(wd_ready, f - 1)
                            else:
                                act.wait_ge(mux_ready, f * 14 + 7 * c + LEAF_AFTER[j])
                            dst = wbuf[:, par, c * HALF:(c + 1) * HALF] if j == 0 else leaf[:, LEAF_BUF[j] - 1, :]
                            A(dst, bits[:, 0, :], ACT.Identity, bias=table[:, 2 * j:2 * j + 1],
                              scale=table_gap[:, j:j + 1]).then_inc(leaf_ready, 1)

                def silus(f):
                    for tb in range(TB):
                        act.wait_ge(gate_up_out, f * 4 + tb + 1)
                        act.wait_ge(h_ready, f * 4 + max(tb - 1, 0) if tb < 2 else f * 4 + tb - 1)
                        A(silu[:, tb % 2, :], banks[:, 2 * tb, :], ACT.Silu).then_inc(silu_ready, 1)

                act.wait_ge(gap_ready, 1)
                leaves(0, 0, first=True)
                leaves(1, 1, first=True)
                silus(0)
                with act.Fori(1, FT - 2, 2) as f:
                    leaves(f + 1, 0)
                    silus(f)
                    leaves(f + 2, 1)
                    silus(f + 1)
                leaves(FT - 1, 0)
                silus(FT - 2)
                silus(FT - 1)
                for t in range(TT):
                    act.wait_ge(shift4_ready, t + 1)
                    A(res[:, t % RR, :], res[:, t % RR, :], ACT.Identity, bias=shift[:, t % 4:t % 4 + 1],
                      scale=rstd[:, t % 4:t % 4 + 1]).then_inc(out_ready, 1)

            @block.vector
            def _(dve):
                V = nc.vector

                def gate_y(b):
                    dve.wait_ge(gate_ready, b + 1)
                    dve.wait_ge(y_in, 16 * b + 16)
                    V.tensor_tensor(yb[b], yb[b], gate[b % 2], ALU.mult).then_inc(gated, 1)

                def residual(b):
                    for lt in range(4):
                        dve.wait_ge(yT_out, b * 4 + lt + 1)
                        V.tensor_tensor(x1b[b][:, lt, :], banks[:, lt, :], x1b[b][:, lt, :], ALU.add)\
                            .then_inc(sum_ready, 1)
                    for lt in range(4):
                        dve.wait_ge(sum_ready, b * 4 + lt + 1)
                        V.bn_stats(stats[:, lt, :], x1b[b][:, lt, :]).then_inc(stat_ready, 1)
                    for lt in range(4):
                        dve.wait_ge(stat_ready, b * 4 + lt + 1)
                        V.bn_aggr(meanvar[:, lt, :], stats[:, lt, :]).then_inc(mv_ready, 1)
                    dve.wait_ge(mv_ready, b * 4 + 4)
                    V.tensor_scalar(vareps[:], meanvar[:, :, 1], EPS, None, ALU.add).then_inc(ve_ready, 1)
                    dve.wait_ge(rstd_ready, b + 1)
                    V.scalar_tensor_tensor(shift[:], meanvar[:, :, 0], -1.0, rstd[:], ALU.mult, ALU.mult)\
                        .then_inc(shift_ready, 1)

                def keep_x2T(b):
                    for ht in range(2, 4):
                        dve.wait_ge(x2T_out, b * 4 + ht + 1)
                        V.tensor_copy(x2T[:, ht, b * 512:(b + 1) * 512], banks[:, 4 + ht, :]).then_inc(x2T_dve, 1)

                dve.wait_ge(lut_in, 16)
                pairs = table[:].rearrange("p (j two) -> p j two", two=2)
                V.tensor_tensor(table_gap[:], pairs[:, :, 1], pairs[:, :, 0], ALU.subtract).then_inc(gap_ready, 1)
                gate_y(0)
                gate_y(1)
                for b in range(S):
                    residual(b)
                    if b + 2 < S:
                        gate_y(b + 2)
                    keep_x2T(b)

                def decode(f, par):
                    for c in range(2):
                        dve.wait_ge(idx_in, f * 16 + 16)
                        dve.wait_ge(leaf_ready, f * 16 + 8 * c)
                        dve.wait_ge(mux_ready, f * 14 + 7 * c)
                        for k in range(4):
                            V.tensor_scalar(bits[:, k, :], idx_sb[:, par, c * HALF:(c + 1) * HALF], 1 << k, None,
                                            ALU.bitwise_and).then_inc(bits_ready, 1)
                        at = lambda n: wbuf[:, par, c * HALF:(c + 1) * HALF] if n == 0 else leaf[:, n - 1, :]
                        for m, (kept, other, bit) in enumerate(MUX):
                            dve.wait_ge(leaf_ready, f * 16 + 8 * c + MUX_LEAVES[m])
                            dve.wait_ge(bits_ready, f * 8 + 4 * c + 4)
                            if m:
                                dve.wait_ge(mux_ready, f * 14 + 7 * c + m)
                            V.memset(wait_here[:], 0.0)
                            V.copy_predicated(at(kept), bits[:, bit, :], at(other)).then_inc(mux_ready, 1)

                def inner(f):
                    for tb in range(TB):
                        dve.wait_ge(silu_ready, f * 4 + tb + 1)
                        V.tensor_tensor(hT[:, f, tb * 512:(tb + 1) * 512], silu[:, tb % 2, :],
                                        banks[:, 2 * tb + 1, :], ALU.mult).then_inc(h_ready, 1)

                decode(0, 0)
                decode(1, 1)
                dve.wait_ge(x2_out, 16 * S)
                inner(0)
                with dve.Fori(1, FT - 2, 2) as f:
                    decode(f + 1, 0)
                    inner(f)
                    decode(f + 2, 1)
                    inner(f + 1)
                decode(FT - 1, 0)
                inner(FT - 2)
                inner(FT - 1)

                for t in range(TT):
                    r = res[:, t % RR, :]
                    j = t % 4
                    dve.wait_ge(down_out, t + 1)
                    dve.wait_ge(x2_in, 16 * t + 16)
                    V.tensor_tensor(r, banks[:, t % 8, :], r, ALU.add).then_inc(res_ready, 1)
                    dve.wait_ge(res_ready, t + 1)
                    V.bn_stats(stats[:, j, :], r).then_inc(stat4_ready, 1)
                    dve.wait_ge(stat4_ready, t + 1)
                    V.bn_aggr(meanvar[:, j, :], stats[:, j, :]).then_inc(mv4_ready, 1)
                    dve.wait_ge(mv4_ready, t + 1)
                    V.tensor_scalar(vareps[:, j:j + 1], meanvar[:, j, 1:2], EPS, None, ALU.add)\
                        .then_inc(ve4_ready, 1)
                    dve.wait_ge(rstd4_ready, t + 1)
                    V.scalar_tensor_tensor(shift[:, j:j + 1], meanvar[:, j, 0:1], -1.0, rstd[:, j:j + 1],
                                           ALU.mult, ALU.mult).then_inc(shift4_ready, 1)

            @block.gpsimd
            def _(pool):
                G = nc.gpsimd
                for b in range(S):
                    pool.wait_ge(ve_ready, b + 1)
                    if b:
                        pool.wait_ge(x2_ready, 4 * b)
                    G.tensor_tensor(rstd[:], vareps[:], minus_half[:], ALU.pow).then_inc(rstd_ready, 1)

                def keep_down(f, par):
                    pool.wait_ge(mux_ready, f * 14 + 14)
                    G.tensor_copy(wd[:, f, :], wbuf[:, par, 2 * H:]).then_inc(wd_ready, 1)

                keep_down(0, 0)
                with pool.Fori(1, FT - 1, 2) as f:
                    keep_down(f, 1)
                    keep_down(f + 1, 0)
                for t in range(TT):
                    j = t % 4
                    pool.wait_ge(ve4_ready, t + 1)
                    if t >= 4:
                        pool.wait_ge(out_ready, t - 3)
                    G.tensor_tensor(rstd[:, j:j + 1], vareps[:, j:j + 1], minus_half[:, j:j + 1], ALU.pow)\
                        .then_inc(rstd4_ready, 1)


def kernel(**inputs):
    import numpy as np
    import ml_dtypes
    import concourse.bacc as bacc
    from concourse.bass_utils import run_bass_kernel_spmd

    def arr(name):
        return np.asarray(inputs[name])

    x = arr("x")
    wqkv = arr("L0_attn_weight_qkv").reshape(4, QT + 2, HD, H)
    wp = arr("L0_attn_weight_proj").reshape(H, 4, QT, HD)
    per_channel = np.concatenate([
        arr("L0_xattn_conv_w"), arr("L0_xattn_conv_b")[:, None], arr("L0_xattn_dt_proj_b")[:, None],
        arr("L0_xattn_D")[:, None], arr("L0_xattn_A_log")], axis=1)
    xp = arr("L0_xattn_x_proj_w")

    def tiles(w):
        return np.concatenate([w, w[:FT * P - F]], axis=0).reshape(FT, P, H)

    gate_up = [tiles(arr(n)).transpose(0, 2, 1).reshape(FT, HT, P, P).transpose(0, 2, 1, 3).reshape(FT, P, H)
               for n in ("L0_ffn_gate_idx", "L0_ffn_up_idx")]
    down = tiles(arr("L0_ffn_down_idx").T)

    rows = np.arange(P)
    headsum = np.zeros((P, QT, 32), np.float32)
    for qt in range(QT):
        headsum[rows, qt, 4 * qt + rows // HD] = 1
    spread = np.zeros((P, S * QT, P), np.float32)
    for i in range(S):
        for qt in range(QT):
            spread[32 * i + 4 * qt + rows // HD, i * QT + qt, rows] = 1
    pick = np.tile(np.eye(32), (3, 1)).astype(ml_dtypes.bfloat16)

    arrays = {
        "xT": x.transpose(2, 0, 1).reshape(H, S * L),
        "x": x,
        "ctxT": arr("ctx_1024").transpose(2, 0, 1).reshape(DM, S * L),
        "wqkvT": wqkv.transpose(1, 0, 2, 3).reshape(6 * P, H).T,
        "wpT": wp.transpose(2, 1, 3, 0).reshape(H, H),
        "ipT": arr("L0_xattn_in_proj_w").T,
        "chan": per_channel.reshape(ET, P, -1).transpose(1, 0, 2),
        "xpT": np.concatenate([xp[DR:], xp[:DR]], axis=0).T,
        "dtT": arr("L0_xattn_dt_proj_w").T,
        "lut": arr("L0_ffn_lut").reshape(1, 16),
        "idx": np.concatenate(gate_up + [down], axis=2),
        "ident_c": np.eye(P, dtype=np.float32),
        "headsum_c": headsum,
        "spread_c": spread,
        "pick_c": pick,
    }
    nc = bacc.Bacc("TRN2", target_bir_lowering=False, num_devices=1)
    args = {}
    for name, a in arrays.items():
        a = arrays[name] = np.ascontiguousarray(a)
        args[name] = nc.dram_tensor(f"in_{name}", a.shape, mybir.dt.from_np(a.dtype), kind="ExternalInput").ap()
    out = nc.dram_tensor("out_0", (S, L, H), mybir.dt.float32, kind="ExternalOutput").ap()
    decoder_kernel(nc, out=out, **args)
    r = run_bass_kernel_spmd(nc, [{f"in_{n}": a for n, a in arrays.items()}], core_ids=[0])
    return r.results[0]["out_0"]
```

```python
import concourse.bass as bass
from concourse import mybir
from contextlib import ExitStack

S, L, H = 4, 512, 512
QT, HD = 4, 32
DM, DI, DS, DR, TAPS = 256, 512, 16, 16, 4
P = 128
LQ = L // S
ET = DI // P
HT = H // P
NG = 4
NQ = DS // NG
STEPS = NQ * ET
RING = 4
F = 1376
FT = -(-F // P)
FLAST = F - (FT - 1) * P
WCH = 2 * H + H
HALF = WCH // 2
EPS = 1e-5
MASKED = -1e30
PRIMED = 1

def decoder_kernel(nc, xT, x, ctxT, wqkvT, wpT, ipT, chan, xpT, dtT, lut, idx, ident_c, headsum_c, spread_c,
                   pick_c, out):
    f32, bf16, i32 = mybir.dt.float32, mybir.dt.bfloat16, mybir.dt.int32
    ALU, ACT, AX = mybir.AluOpType, mybir.ActivationFunctionType, mybir.AxisListType

    x1_scratch = nc.dram_tensor("x1_scratch", [S, L, H], f32, kind="Internal").ap()
    y_scratch = nc.dram_tensor("y_scratch", [S, DI, L], f32, kind="Internal").ap()
    x2_scratch = nc.dram_tensor("x2_scratch", [S, L, H], f32, kind="Internal").ap()

    top = ExitStack()
    with top:
        def sem(name, ctx=top):
            return ctx.enter_context(nc.semaphore(name))

        ident = top.enter_context(nc.sbuf_tensor("ident", [P, P], f32))
        banks = top.enter_context(nc.psum_tensor("banks", [P, 8, 512], f32))
        stats = top.enter_context(nc.sbuf_tensor("stats", [P, 4, 6], f32))
        meanvar = top.enter_context(nc.sbuf_tensor("meanvar", [P, 4, 2], f32))
        vareps = top.enter_context(nc.sbuf_tensor("vareps", [P, 4], f32))
        rstd = top.enter_context(nc.sbuf_tensor("rstd", [P, 4], f32))
        shift = top.enter_context(nc.sbuf_tensor("shift", [P, 4], f32))
        minus_half = top.enter_context(nc.sbuf_tensor("minus_half", [P, 4], f32))

        stage1(nc, top, ident, banks, (stats, meanvar, vareps, rstd, shift, minus_half), xT, x, ctxT, wqkvT, wpT,
               ipT, chan, xpT, dtT, ident_c, headsum_c, spread_c, pick_c, x1_scratch, y_scratch)
        stage234(nc, top, ident, banks, (stats, meanvar, vareps, rstd, shift, minus_half), lut, idx,
                 x1_scratch, y_scratch, x2_scratch, out)


def stage1(nc, top, ident, banks, ln, xT, x, ctxT, wqkvT, wpT, ipT, chan, xpT, dtT, ident_c, headsum_c,
           spread_c, pick_c, x1_scratch, y_scratch):
    f32, bf16 = mybir.dt.float32, mybir.dt.bfloat16
    ALU, ACT, AX = mybir.AluOpType, mybir.ActivationFunctionType, mybir.AxisListType
    stats, meanvar, vareps, rstd, shift, minus_half = ln
    ctx = ExitStack()
    with ctx:
        def sb(name, shape, dt=f32):
            return ctx.enter_context(nc.sbuf_tensor(name, shape, dt))

        def sem(name):
            return ctx.enter_context(nc.semaphore(name))

        wqkv = sb("wqkv", [P, HT, 6 * P])
        wp = sb("wp", [P, QT, H])
        ip = sb("ip", [P, DM // P, DI])
        ch = sb("ch", [P, ET, TAPS + 3 + DS])
        xp_w = sb("xp_w", [P, ET, 3 * DS])
        dt_w = sb("dt_w", [DR, DI])
        headsum = sb("headsum", [P, QT, 32])
        spread = sb("spread", [P, S * QT, P])
        pick = sb("pick", [96, 32], bf16)
        negA = sb("negA", [P, ET, DS])
        ctx_sb = sb("ctx_sb", [P, DM // P, L])
        xT_sb = sb("xT_sb", [P, HT, S, LQ])
        x_sb = sb("x_sb", [P, S, H])
        q = sb("q", [P, QT, S, LQ])
        kv = sb("kv", [P, 2, S, LQ])
        prod_b = sb("prod_b", [P, QT, S - 1, LQ])
        prob = sb("prob", [P, S, LQ])
        rowmax = sb("rowmax", [P, LQ])
        rowsum = sb("rowsum", [P, LQ])
        rowinv = sb("rowinv", [P, LQ])
        conv_in = sb("conv_in", [P, ET, TAPS - 1 + L])
        u = sb("u", [P, ET, L])
        bc_parts = sb("bc_parts", [96, L], bf16)
        bc_rest = sb("bc_rest", [32, L])
        bc_mid = sb("bc_mid", [32, L], bf16)
        dt_lo = sb("dt_lo", [DR, L])
        delta = sb("delta", [P, ET, L])
        du = sb("du", [P, ET, L])
        brep = sb("brep", [P, 2, NG, L])
        crep = sb("crep", [P, 2, NG, L])
        decay = sb("decay", [P, 2, NG, L])
        state = sb("state", [P, RING, NG, L])
        y_sb = sb("y_sb", [P, ET, L])
        conv_w = lambda et, j: ch[:, et, j:j + 1]
        conv_b = lambda et: ch[:, et, TAPS:TAPS + 1]
        dt_b = lambda et: ch[:, et, TAPS + 1:TAPS + 2]
        skip_d = lambda et: ch[:, et, TAPS + 2:TAPS + 3]
        a_log = ch[:, :, TAPS + 3:TAPS + 3 + DS]
        k, v = kv[:, 0], kv[:, 1]
        conv_acc, expneg, relu = state[:, 0], state[:, 1], state[:, 2]
        prod_a = state[:, 3].rearrange("p t (s l) -> p t s l", s=S)
        prod = [prod_b[:, :, 0:1, :], prod_a[:, :, 0:2, :], prod_b[:, :, 0:3, :], prod_a]
        pv = [prod_b[:, :, 0:1, :].rearrange("p t s l -> p (t s) l"), prod_b[:, :, 1:2, :].rearrange("p t s l -> p (t s) l")]

        (ip_in, w_in, ctx_in, xT_in, x_in, negA_ready, setup_done, inproj_out, qkv_out, bc_out, dt_out,
         delta_out, score_out, rep_out, pb_out, proj_out, nsum_done, xp_ready, qkv_ready, conv_tap, u_ready,
         bc_hi, bc_r1, bc_m, bc_lo, dtlo_ready, abs_ready, expneg_ready, onep_ready, ln_ready, corr_ready,
         base_ready, relu_ready, delta_ready, du_ready, prod_ready, masked, max_ready, sub_ready, exp_ready,
         sum_ready, inv_ready, prob_ready, pv_mul, pv_sum, rep_ready, decay_ready, dbu_ready, scan_ready,
         hc_ready, res_ready, stat_ready, mv_ready, ve_ready, rstd_ready, shift_ready, x1_ready, x1_out,
         y_ready, y_out, half_ready) = [sem(n) for n in (
             "ip_in w_in ctx_in xT_in x_in negA_ready setup_done inproj_out qkv_out bc_out dt_out "
             "delta_out score_out rep_out pb_out proj_out nsum_done xp_ready qkv_ready conv_tap u_ready "
             "bc_hi bc_r1 bc_m bc_lo dtlo_ready abs_ready expneg_ready onep_ready ln_ready corr_ready "
             "base_ready relu_ready delta_ready du_ready prod_ready masked max_ready sub_ready exp_ready "
             "sum_ready inv_ready prob_ready pv_mul pv_sum rep_ready decay_ready dbu_ready scan_ready "
             "hc_ready res_ready stat_ready mv_ready ve_ready rstd_ready shift_ready x1_ready x1_out "
             "y_ready y_out half_ready").split()]
        N_W = 8
        PB_AT = {t: (2 * t - 4, 2 * t - 3) for t in range(2, 10)}
        PV_AT = {t + 2: ns for t, ns in PB_AT.items()}
        PROJ_AT = {12: 0, 13: 1, 14: 2, 15: 3}
        RES_AT = {14: (0,), 15: (1, 2, 3)}

        with nc.Block() as block:

            @block.sync
            def _(sp):
                sp.dma_start(ip[:], ipT.rearrange("(t p) n -> p t n", p=P)).then_inc(ip_in, 16)
                sp.dma_start(ch[:], chan).then_inc(ip_in, 16)

                def load(b, first=False):
                    if not first:
                        sp.wait_ge(inproj_out, b * ET)
                    sp.dma_start(ctx_sb[:], ctxT.rearrange("(t p) (b l) -> p t b l", p=P, b=S)[:, :, b, :])\
                        .then_inc(ctx_in, 16)
                    if not first:
                        sp.wait_ge(qkv_out, b * 6)
                    for t in range(HT):
                        sp.dma_start(xT_sb[:, t], xT.rearrange("(t p) (s c l) -> t p s c l", p=P, s=S, c=S)[t, :, :, b, :])\
                            .then_inc(xT_in, 16)
                    if not first:
                        sp.wait_ge(x1_out, b * 16)
                    sp.dma_start(x_sb[:], x.rearrange("s (c p) h -> p s c h", p=P)[:, :, b, :]).then_inc(x_in, 16)

                load(0, first=True)
                with sp.Fori(1, S) as b:
                    load(b)


            @block.tensor
            def _(pe):
                mm = nc.tensor.matmul
                pe.sem_inc(nsum_done, PRIMED)
                pe.wait_ge(ip_in, 32)
                with pe.Fori(0, S) as b:
                    pe.wait_ge(ctx_in, b * 16 + 16)
                    pe.wait_ge(res_ready, PRIMED + b * S)
                    pe.wait_ge(rep_ready, PRIMED + b * 2 * DS)
                    for et in range(ET):
                        for t in range(DM // P):
                            last = mm(banks[:, et, :], ip[:, t, et * P:(et + 1) * P], ctx_sb[:, t, :],
                                      start=t == 0, stop=t == DM // P - 1)
                        last.then_inc(inproj_out, 1)

                    def qkv(m):
                        if m >= 4:
                            pe.wait_ge(qkv_ready, b * 6 + m - 3)
                        for t in range(HT):
                            last = mm(banks[:, 4 + m % 4, :], wqkv[:, t, m * P:(m + 1) * P],
                                      xT_sb[:, t].rearrange("p s l -> p (s l)"), start=t == 0, stop=t == HT - 1)
                        last.then_inc(qkv_out, 1)

                    pe.wait_ge(w_in, N_W * 16)
                    pe.wait_ge(xT_in, b * 64 + 64)
                    pe.wait_ge(y_ready, PRIMED + b * ET)
                    qkv(0)
                    qkv(1)
                    qkv(2)
                    pe.wait_ge(xp_ready, b * ET + 2)
                    pe.wait_ge(u_ready, b * ET + ET)
                    for et in range(ET):
                        last = mm(banks[0:DR, 1, :], xp_w[:, et, 2 * DS:3 * DS], u[:, et, :],
                                  start=et == 0, stop=et == ET - 1)
                    last.then_inc(dt_out, 1)
                    for et in range(ET):
                        last = mm(banks[0:2 * DS, 0, :], xp_w[:, et, 0:2 * DS], u[:, et, :],
                                  start=et == 0, stop=et == ET - 1)
                    last.then_inc(bc_out, 1)
                    pe.wait_ge(xp_ready, b * ET + 4)
                    pe.wait_ge(dtlo_ready, b + 1)
                    for et in (1, 2, 3, 0):
                        if et == 0:
                            pe.wait_ge(bc_r1, b + 1)
                        mm(banks[:, et, :], dt_w[:, et * P:(et + 1) * P], dt_lo[:],
                           start=True, stop=True).then_inc(delta_out, 1)
                    qkv(3)
                    qkv(4)
                    qkv(5)

                    def repeat_rows(g, rs):
                        for r in rs:
                            if g == 0:
                                bank = 6 + r % 2
                                if r < 2:
                                    pe.wait_ge(qkv_ready, b * 6 + 3 + r)
                            else:
                                bank = 2 + r % 2
                                if g == 1 and r < 2:
                                    pe.wait_ge(relu_ready, b * ET + ET)
                            if g or r >= 2:
                                pe.wait_ge(rep_ready, PRIMED + b * 2 * DS + 2 * NG * g + r - 1)
                            row = (DS if r >= NG else 0) + NG * g + r % NG
                            mm(banks[:, bank, :], pick[:, row:row + 1].to_broadcast([96, P]), bc_parts[:],
                               start=True, stop=True).then_inc(rep_out, 1)

                    pe.wait_ge(bc_lo, b + 1)
                    pe.wait_ge(bc_m, b * 2 + 2)
                    repeat_rows(0, range(2 * NG))
                    pe.wait_ge(relu_ready, b * ET + ET)
                    for i in range(S):
                        pe.wait_ge(prod_ready, b * S + i + 1)
                        for qt in range(QT):
                            last = mm(banks[32 * i:32 * i + 32, 0, 0:(i + 1) * LQ], headsum[:, qt, :],
                                      prod[i][:, qt].rearrange("p j l -> p (j l)"),
                                      start=qt == 0, stop=qt == QT - 1)
                        last.then_inc(score_out, 1)

                    def repeat_probs(n):
                        i, qt = divmod(n, QT)
                        if n == 0:
                            pe.wait_ge(prob_ready, b + 1)
                        if n >= 2:
                            pe.wait_ge(pv_mul, b * 16 + n - 1)
                        mm(banks[:, n % 2, 0:(i + 1) * LQ], spread[:, n, :],
                           prob[:, 0:i + 1, :].rearrange("p j l -> p (j l)"), start=True, stop=True)\
                            .then_inc(pb_out, 1)

                    def project(s):
                        if s == 0:
                            pe.wait_ge(pv_sum, PRIMED + b * 16 + 16)
                        elif s >= 2:
                            pe.wait_ge(res_ready, PRIMED + b * S + s - 1)
                        for qt in range(QT):
                            last = mm(banks[:, s % 2, :], q[:, qt, s, :], wp[:, qt, :],
                                      start=qt == 0, stop=qt == QT - 1)
                        last.then_inc(proj_out, 1)

                    for t in range(STEPS):
                        g, et = t // ET, t % ET
                        if g < NQ - 1 and (t == 0 or et < 3 and t > 0):
                            if t == 0:
                                repeat_rows(1, (0, 1))
                            repeat_rows(g + 1, (2 * et + 2, 2 * et + 3))
                        if et == 3 and g + 2 < NQ:
                            repeat_rows(g + 2, (0, 1))
                        if t in PB_AT:
                            for n in PB_AT[t]:
                                repeat_probs(n)
                        if t in PROJ_AT:
                            project(PROJ_AT[t])
                        if t == 0:
                            pe.wait_ge(qkv_ready, b * 6 + 6)
                            pe.wait_ge(rep_ready, PRIMED + b * 2 * DS + 2 * NG)
                        pe.wait_ge(hc_ready, PRIMED + b * STEPS + t + 1)
                        for n in range(NG):
                            last = mm(banks[:, 4 + et, :], ident[:], state[:, t % RING, n, :],
                                      start=(g == 0 and n == 0), stop=(g == NQ - 1 and n == NG - 1))
                        last.then_inc(nsum_done, 1)

            @block.scalar
            def _(act):
                A = nc.scalar.activation
                act.dma_start(wqkv[:], wqkvT.rearrange("(t p) n -> p t n", p=P)).then_inc(w_in, 16)
                act.dma_start(xp_w[:], xpT.rearrange("(t p) n -> p t n", p=P)).then_inc(w_in, 16)
                act.dma_start(dt_w[:], dtT).then_inc(w_in, 16)
                act.dma_start(pick[:], pick_c).then_inc(w_in, 16)
                act.dma_start(headsum[:], headsum_c).then_inc(w_in, 16)
                act.dma_start(spread[:], spread_c).then_inc(w_in, 16)
                act.dma_start(wp[:], wpT.rearrange("(t p) n -> p t n", p=P)).then_inc(w_in, 16)
                act.dma_start(ident[:], ident_c).then_inc(w_in, 16)
                act.wait_ge(ip_in, 32)
                A(negA[:], a_log, ACT.Exp).then_inc(negA_ready, 1)
                act.sem_inc(rep_ready, PRIMED)
                act.wait_ge(setup_done, 4)
                with act.Fori(0, S) as b:
                    act.wait_ge(conv_tap, PRIMED + b * 16)
                    for et in range(ET):
                        act.wait_ge(inproj_out, b * ET + et + 1)
                        A(conv_in[:, et, TAPS - 1:], banks[:, et, :], ACT.Copy).then_inc(xp_ready, 1)

                    def keep_qkv(m):
                        act.wait_ge(qkv_out, b * 6 + m + 1)
                        dst = q[:, m] if m < QT else kv[:, m - QT]
                        A(dst.rearrange("p s l -> p (s l)"), banks[:, 4 + m % 4, :], ACT.Copy).then_inc(qkv_ready, 1)

                    act.wait_ge(pv_sum, PRIMED + b * 16)
                    act.wait_ge(res_ready, PRIMED + b * S)
                    act.wait_ge(y_ready, PRIMED + b * ET)
                    keep_qkv(0)
                    for et in range(ET):
                        act.wait_ge(conv_tap, PRIMED + b * 16 + 12 + et + 1)
                        A(u[:, et, :], conv_acc[:, et, :], ACT.Silu).then_inc(u_ready, 1)
                    keep_qkv(1)
                    keep_qkv(2)
                    act.wait_ge(dt_out, b + 1)
                    A(dt_lo[:], banks[0:DR, 1, :], ACT.Copy).then_inc(dtlo_ready, 1)
                    act.wait_ge(bc_out, b + 1)
                    A(bc_parts[0:32, :], banks[0:32, 0, :], ACT.Copy).then_inc(bc_hi, 1)
                    act.wait_ge(nsum_done, PRIMED + b * STEPS)
                    for n, et in enumerate((1, 2, 3, 0)):
                        if et == 0:
                            act.wait_ge(bc_r1, b + 1)
                            A(bc_mid[:], bc_rest[:], ACT.Copy).then_inc(bc_m, 1)
                            A(bc_parts[32:64, :], bc_rest[:], ACT.Copy).then_inc(bc_m, 1)
                        act.wait_ge(delta_out, b * ET + n + 1)
                        A(expneg[:, et, :], banks[:, et, :], ACT.Abs, bias=dt_b(et)).then_inc(abs_ready, 1)
                    act.wait_ge(abs_ready, b * ET + ET)
                    A(expneg[:], expneg[:], ACT.Exp, scale=-1.0).then_inc(expneg_ready, 1)
                    keep_qkv(3)
                    act.wait_ge(onep_ready, b + 1)
                    A(delta[:], conv_acc[:], ACT.Ln).then_inc(ln_ready, 1)
                    keep_qkv(4)
                    keep_qkv(5)

                    def keep_rows(g, rs):
                        for r in rs:
                            act.wait_ge(rep_out, b * 2 * DS + 2 * NG * g + r + 1)
                            dst = brep if r < NG else crep
                            bank = 6 + r % 2 if g == 0 else 2 + r % 2
                            A(dst[:, g % 2, r % NG, :], banks[:, bank, :], ACT.Copy).then_inc(rep_ready, 1)

                    act.wait_ge(dbu_ready, PRIMED + b * STEPS)
                    act.wait_ge(hc_ready, PRIMED + b * STEPS)
                    keep_rows(0, range(2 * NG))
                    act.wait_ge(delta_ready, b + 1)
                    for t in range(STEPS):
                        g, et = t // ET, t % ET
                        act.wait_ge(scan_ready, PRIMED + b * STEPS + max(t - 1, 0))
                        for n in range(NG):
                            A(decay[:, t % 2, n, 1:], delta[:, et, 1:], ACT.Exp,
                              scale=negA[:, et, NG * g + n:NG * g + n + 1]).then_inc(decay_ready, 1)
                        if et in (2, 3) and g < NQ - 1:
                            keep_rows(g + 1, range(2 * (et - 2), 2 * (et - 1)))
                        if et in (0, 1) and g:
                            act.wait_ge(hc_ready, PRIMED + b * STEPS + ET * (g - 1))
                            keep_rows(g, range(4 + 2 * et, 6 + 2 * et))
                        if t == 2:
                            act.wait_ge(sub_ready, b + 1)
                            A(prob[:], prob[:], ACT.Exp, scale=float(HD) ** -0.5).then_inc(exp_ready, 1)

            @block.vector
            def _(dve):
                V = nc.vector
                V.memset(decay[:, :, :, 0:1], 0.0).then_inc(setup_done, 1)
                V.memset(conv_in[:, :, 0:TAPS - 1], 0.0).then_inc(setup_done, 1)
                V.memset(prob[:], 0.0).then_inc(setup_done, 1)
                dve.wait_ge(negA_ready, 1)
                V.tensor_scalar(negA[:], negA[:], -1.0, None, ALU.mult).then_inc(setup_done, 1)
                for primed in (res_ready, y_ready, conv_tap, pv_sum, dbu_ready, scan_ready):
                    dve.sem_inc(primed, PRIMED)
                with dve.Fori(0, S) as b:
                    dve.wait_ge(nsum_done, PRIMED + b * STEPS)
                    for j in range(TAPS):
                        for et in range(ET):
                            tap = conv_in[:, et, j:j + L]
                            if j == 0:
                                dve.wait_ge(xp_ready, b * ET + et + 1)
                                V.tensor_scalar(conv_acc[:, et, :], tap, conv_w(et, 0), conv_b(et), ALU.mult,
                                                ALU.add).then_inc(conv_tap, 1)
                            else:
                                dve.wait_ge(conv_tap, PRIMED + b * 16 + 4 * (j - 1) + et + 1)
                                V.scalar_tensor_tensor(conv_acc[:, et, :], tap, conv_w(et, j), conv_acc[:, et, :],
                                                       ALU.mult, ALU.add).then_inc(conv_tap, 1)

                    dve.wait_ge(bc_hi, b + 1)
                    V.tensor_tensor(bc_rest[:], banks[0:32, 0, :], bc_parts[0:32, :], ALU.subtract).then_inc(bc_r1, 1)
                    for n, et in enumerate((1, 2, 3, 0)):
                        dve.wait_ge(abs_ready, b * ET + n + 1)
                        V.tensor_scalar(relu[:, et, :], banks[:, et, :], dt_b(et), 0.0, ALU.add, ALU.max)\
                            .then_inc(relu_ready, 1)
                    dve.wait_ge(bc_r1, b + 1)
                    dve.wait_ge(bc_m, b * 2 + 1)
                    V.tensor_tensor(bc_parts[64:96, :], bc_rest[:], bc_mid[:], ALU.subtract).then_inc(bc_lo, 1)
                    dve.wait_ge(expneg_ready, b + 1)
                    V.tensor_scalar(conv_acc[:], expneg[:], 1.0, None, ALU.add).then_inc(onep_ready, 1)
                    dve.wait_ge(onep_ready, b + 1)
                    V.scalar_tensor_tensor(expneg[:], conv_acc[:], -1.0, expneg[:], ALU.add, ALU.subtract)\
                        .then_inc(corr_ready, 1)
                    dve.wait_ge(corr_ready, b + 1)
                    dve.wait_ge(relu_ready, b * ET + ET)
                    V.tensor_tensor(relu[:], relu[:], expneg[:], ALU.subtract).then_inc(base_ready, 1)
                    dve.wait_ge(base_ready, b + 1)
                    dve.wait_ge(ln_ready, b + 1)
                    V.tensor_tensor(delta[:], delta[:], relu[:], ALU.add).then_inc(delta_ready, 1)

                    def score_product(i):
                        if i >= 2:
                            dve.wait_ge(score_out, b * S + i - 1)
                        shape = [P, QT, i + 1, LQ]
                        V.tensor_tensor(prod[i], q[:, :, i:i + 1, :].to_broadcast(shape),
                                        k[:, 0:i + 1, :].unsqueeze(1).to_broadcast(shape), ALU.mult)\
                            .then_inc(prod_ready, 1)

                    dve.wait_ge(qkv_ready, b * 6 + 5)
                    for i in range(S):
                        score_product(i)

                    def softmax_difference():
                        dve.wait_ge(score_out, b * S + S)
                        for i in range(S - 1):
                            V.memset(banks[32 * i:32 * i + 32, 0, (i + 1) * LQ:], MASKED).then_inc(masked, 1)
                        dve.wait_ge(masked, b * 3 + 3)
                        sc = banks[:, 0, :].rearrange("p (j l) -> p j l", j=S)
                        V.tensor_reduce(rowmax[:], sc.rearrange("p j l -> p l j"), AX.X, ALU.max).then_inc(max_ready, 1)
                        dve.wait_ge(max_ready, b + 1)
                        V.tensor_tensor(prob[:], sc, rowmax[:].unsqueeze(1).to_broadcast([P, S, LQ]), ALU.subtract)\
                            .then_inc(sub_ready, 1)

                    def softmax_quotient():
                        dve.wait_ge(exp_ready, b + 1)
                        V.tensor_reduce(rowsum[:], prob[:].rearrange("p j l -> p l j"), AX.X, ALU.add)\
                            .then_inc(sum_ready, 1)
                        dve.wait_ge(sum_ready, b + 1)
                        V.reciprocal(rowinv[:], rowsum[:]).then_inc(inv_ready, 1)
                        dve.wait_ge(inv_ready, b + 1)
                        V.tensor_tensor(prob[:], prob[:], rowinv[:].unsqueeze(1).to_broadcast([P, S, LQ]), ALU.mult)\
                            .then_inc(prob_ready, 1)

                    def pv_product(n):
                        i, qt = divmod(n, QT)
                        dve.wait_ge(pb_out, b * 16 + n + 1)
                        if n == 0:
                            dve.wait_ge(qkv_ready, b * 6 + 6)
                        if n >= 2:
                            dve.wait_ge(pv_sum, PRIMED + b * 16 + n - 1)
                        V.tensor_tensor(pv[n % 2][:, 0:i + 1, :],
                                        banks[:, n % 2, 0:(i + 1) * LQ].rearrange("p (j l) -> p j l", l=LQ),
                                        v[:, 0:i + 1, :], ALU.mult).then_inc(pv_mul, 1)

                    def pv_total(n):
                        i, qt = divmod(n, QT)
                        dve.wait_ge(pv_mul, b * 16 + n + 1)
                        V.tensor_reduce(q[:, qt, i, :], pv[n % 2][:, 0:i + 1, :].rearrange("p j l -> p l j"),
                                        AX.X, ALU.add).then_inc(pv_sum, 1)

                    def residual(s):
                        dve.wait_ge(proj_out, b * S + s + 1)
                        if s == 0:
                            dve.wait_ge(x_in, b * 16 + 16)
                        V.tensor_tensor(x_sb[:, s, :], banks[:, s % 2, :], x_sb[:, s, :], ALU.add)\
                            .then_inc(res_ready, 1)
                        dve.wait_ge(res_ready, PRIMED + b * S + s + 1)
                        V.bn_stats(stats[:, s, :], x_sb[:, s, :]).then_inc(stat_ready, 1)
                        dve.wait_ge(setup_done, 4)
                        dve.wait_ge(stat_ready, b * S + s + 1)
                        V.bn_aggr(meanvar[:, s, :], stats[:, s, :]).then_inc(mv_ready, 1)

                    def input_product(t):
                        g, et = t // ET, t % ET
                        if t >= RING:
                            dve.wait_ge(nsum_done, PRIMED + b * STEPS + t - RING + 1)
                        dve.wait_ge(rep_ready, PRIMED + b * 2 * DS + 2 * NG * g + NG)
                        dve.wait_ge(du_ready, b * ET + min(t, ET - 1) + 1)
                        V.tensor_tensor(state[:, t % RING], du[:, et:et + 1, :].to_broadcast([P, NG, L]),
                                        brep[:, g % 2], ALU.mult).then_inc(dbu_ready, 1)

                    def scan(t):
                        dve.wait_ge(dbu_ready, PRIMED + b * STEPS + t + 1)
                        dve.wait_ge(decay_ready, b * STEPS * NG + NG * t + NG)
                        flat = state[:, t % RING].rearrange("p n l -> p (n l)")
                        V.tensor_tensor_scan(flat, decay[:, t % 2].rearrange("p n l -> p (n l)"), flat, 0.0,
                                             ALU.mult, ALU.add).then_inc(scan_ready, 1)

                    input_product(0)
                    for t in range(STEPS):
                        if t + 1 < STEPS:
                            input_product(t + 1)
                        scan(t)
                        if t == 0:
                            softmax_difference()
                        if t == 2:
                            softmax_quotient()
                        for n in PV_AT.get(t, ()):
                            pv_product(n)
                        for n in PV_AT.get(t, ()):
                            pv_total(n)
                        for s in RES_AT.get(t, ()):
                            residual(s)
                    dve.wait_ge(mv_ready, b * S + S)
                    V.tensor_scalar(vareps[:], meanvar[:, :, 1], EPS, None, ALU.add).then_inc(ve_ready, 1)
                    for et in range(ET):
                        dve.wait_ge(nsum_done, PRIMED + b * STEPS + STEPS - ET + et + 1)
                        V.scalar_tensor_tensor(y_sb[:, et, :], u[:, et, :], skip_d(et), banks[:, 4 + et, :],
                                               ALU.mult, ALU.add).then_inc(y_ready, 1)
                    dve.wait_ge(rstd_ready, b + 1)
                    V.scalar_tensor_tensor(shift[:], meanvar[:, :, 0], -1.0, rstd[:], ALU.mult, ALU.mult)\
                        .then_inc(shift_ready, 1)
                    dve.wait_ge(shift_ready, b + 1)
                    for s in range(S):
                        V.tensor_scalar(x_sb[:, s, :], x_sb[:, s, :], rstd[:, s:s + 1], shift[:, s:s + 1],
                                        ALU.mult, ALU.add).then_inc(x1_ready, 1)

            @block.gpsimd
            def _(pool):
                G = nc.gpsimd
                G.memset(minus_half[:], -0.5).then_inc(half_ready, 1)
                pool.wait_ge(half_ready, 1)
                pool.sem_inc(hc_ready, PRIMED)
                with pool.Fori(0, S) as b:
                    pool.wait_ge(delta_ready, b + 1)
                    for et in range(ET):
                        G.tensor_tensor(du[:, et, :], delta[:, et, :], u[:, et, :], ALU.mult).then_inc(du_ready, 1)
                    for t in range(STEPS):
                        g = t // ET
                        pool.wait_ge(rep_ready, PRIMED + b * 2 * DS + 2 * NG * (g + 1))
                        pool.wait_ge(scan_ready, PRIMED + b * STEPS + t + 1)
                        G.tensor_tensor(state[:, t % RING], state[:, t % RING], crep[:, g % 2], ALU.mult)\
                            .then_inc(hc_ready, 1)
                    pool.wait_ge(ve_ready, b + 1)
                    G.tensor_tensor(rstd[:], vareps[:], minus_half[:], ALU.pow).then_inc(rstd_ready, 1)
                    pool.wait_ge(y_ready, PRIMED + b * ET + ET)
                    pool.dma_start(y_scratch.rearrange("b (t p) l -> p b t l", p=P)[:, b], y_sb[:])\
                        .then_inc(y_out, 16)
                    pool.wait_ge(x1_ready, b * S + S)
                    pool.dma_start(x1_scratch.rearrange("s (c p) h -> p s c h", p=P)[:, :, b, :], x_sb[:])\
                        .then_inc(x1_out, 16)
                    pool.wait_ge(y_out, b * 16 + 16)
                pool.wait_ge(x1_out, 16 * S)


def stage234(nc, top, ident, banks, ln, lut, idx, x1_scratch, y_scratch, x2_scratch, out):
    f32, i32 = mybir.dt.float32, mybir.dt.int32
    ALU, ACT, AX = mybir.AluOpType, mybir.ActivationFunctionType, mybir.AxisListType
    stats, meanvar, vareps, rstd, shift, minus_half = ln
    ctx = ExitStack()
    with ctx:
        def sb(name, shape, dt=f32):
            return ctx.enter_context(nc.sbuf_tensor(name, shape, dt))

        def sem(name):
            return ctx.enter_context(nc.semaphore(name))

        table = sb("table", [P, 16])
        table_gap = sb("table_gap", [P, 8])
        x2T = sb("x2T", [P, HT, S * L])
        hT = sb("hT", [P, FT, S * L])
        wd = sb("wd", [P, FT, H])
        wbuf = sb("wbuf", [P, 2, WCH])
        leaf = sb("leaf", [P, 4, HALF])
        bits = sb("bits", [P, 4, HALF], i32)
        idx_sb = sb("idx_sb", [P, 2, WCH], i32)
        silu = sb("silu", [P, 2, 512])
        wait_here = sb("wait_here", [P, 1])
        res = sb("res", [P, 3, H])
        flat_h = hT[:].rearrange("p f n -> p (f n)")
        x1b = [flat_h[:, b * 2048:(b + 1) * 2048].rearrange("p (t h) -> p t h", h=H) for b in range(S)]
        yb = [flat_h[:, (4 + b) * 2048:(5 + b) * 2048].rearrange("p (t h) -> p t h", h=L) for b in range(S)]
        gate = [flat_h[:, (8 + b) * 2048:(9 + b) * 2048].rearrange("p (t h) -> p t h", h=H) for b in range(2)]

        x1_in = [sem(f"x1_in{b}") for b in range(S)]
        y_in = [sem(f"y_in{b}") for b in range(S)]
        (gate_ready, gated, yT_out, sum_ready, stat_ready, mv_ready, ve_ready, rstd_ready,
         shift_ready, x2_ready, x2_out, x2T_out, x2T_act, x2T_dve, lut_in, gap_ready, idx_in, bits_ready,
         leaf_ready, mux_ready, wd_ready, gate_up_out, silu_ready, h_ready, down_out, x2_in, res_ready,
         stat4_ready, mv4_ready, ve4_ready, rstd4_ready, shift4_ready, out_ready, stored) = [sem(n) for n in (
             "gate_ready gated yT_out sum2_ready stat2_ready mv2_ready ve2_ready rstd2_ready "
             "shift2_ready x2_ready x2_out x2T_out x2T_act x2T_dve lut_in gap_ready idx_in bits_ready "
             "leaf_ready mux_ready wd_ready gate_up_out silu_ready h_ready down_out x2_in res4_ready "
             "stat4_ready mv4_ready ve4_ready rstd4_ready shift4_ready out_ready stored").split()]
        TT = S * L // P
        TB = S * L // 512
        RR = 3

        LEAF_BUF = [0, 1, 2, 3, 1, 3, 2, 4]
        LEAF_AFTER = [None, 0, 0, 0, 1, 2, 3, 0]
        MUX = [(0, 1, 1), (2, 3, 1), (0, 2, 2), (1, 3, 1), (2, 4, 1), (1, 2, 2), (0, 1, 3)]
        MUX_LEAVES = [2, 4, 4, 6, 8, 8, 8]

        with nc.Block() as block:

            @block.sync
            def _(sp):
                sp.dma_start(table[:], lut.to_broadcast([P, 16])).then_inc(lut_in, 16)
                sp.dma_start(idx_sb[:, 0], idx[0]).then_inc(idx_in, 16)
                for b in range(S):
                    sp.dma_start(x1b[b], x1_scratch[b].rearrange("(t p) h -> p t h", p=P)).then_inc(x1_in[b], 16)
                    sp.dma_start(yb[b], y_scratch[b].rearrange("(t p) l -> p t l", p=P)).then_inc(y_in[b], 16)
                sp.wait_ge(idx_in, 16)
                sp.dma_start(idx_sb[:, 1], idx[1]).then_inc(idx_in, 16)
                for b in range(S):
                    sp.wait_ge(x2_ready, b * 4 + 4)
                    sp.dma_start(x2_scratch[b].rearrange("(t p) h -> p t h", p=P), x1b[b]).then_inc(x2_out, 16)
                with sp.Fori(2, FT - 1, 2) as f2:
                    for d in range(2):
                        sp.wait_ge(idx_in, (f2 + d) * 16)
                        sp.wait_ge(bits_ready, (f2 + d) * 8 - 8)
                        sp.dma_start(idx_sb[:, d], idx[f2 + d]).then_inc(idx_in, 16)
                sp.wait_ge(idx_in, (FT - 1) * 16)
                sp.wait_ge(bits_ready, (FT - 1) * 8 - 8)
                sp.dma_start(idx_sb[:, (FT - 1) % 2], idx[FT - 1]).then_inc(idx_in, 16)
                sp.wait_ge(x2_out, 16 * S)
                for t in range(TT + 2):
                    if t < TT:
                        if t >= RR:
                            sp.wait_ge(stored, (t - RR) * 16 + 16)
                        b, c = divmod(t, 4)
                        sp.dma_start(res[:, t % RR, :], x2_scratch[b, c * P:(c + 1) * P, :]).then_inc(x2_in, 16)
                        sp.wait_ge(x2_in, 16 * t + 16)
                    if t >= 2:
                        b, c = divmod(t - 2, 4)
                        sp.wait_ge(out_ready, t - 1)
                        sp.dma_start(out[b, c * P:(c + 1) * P, :], res[:, (t - 2) % RR, :]).then_inc(stored, 16)
                sp.wait_ge(stored, TT * 16)

            @block.tensor
            def _(pe):
                mm = nc.tensor.matmul

                def gated_back(b):
                    pe.wait_ge(gated, b + 1)
                    for lt in range(4):
                        if b:
                            pe.wait_ge(sum_ready, (b - 1) * 4 + lt + 1)
                        for et in range(4):
                            last = nc.tensor.transpose(banks[:, 2 + lt, et * P:(et + 1) * P],
                                                       yb[b][:, et, lt * P:(lt + 1) * P], ident[:])
                        last.then_inc(yT_out, 1)

                def x2_over(b):
                    pe.wait_ge(x2_ready, b * 4 + 4)
                    for ht in range(4):
                        if ht >= 2:
                            pe.wait_ge(x2T_act, b * 2 + ht - 1)
                        elif b:
                            pe.wait_ge(x2T_dve, b * 2 + ht - 1)
                        for lt in range(4):
                            last = nc.tensor.transpose(banks[:, 6 + ht % 2, lt * P:(lt + 1) * P],
                                                       x1b[b][:, lt, ht * P:(ht + 1) * P], ident[:])
                        last.then_inc(x2T_out, 1)

                def gate_up(f, par, blocks=range(TB), first=False):
                    pe.wait_ge(mux_ready, f * 14 + 14)
                    for tb in blocks:
                        if first:
                            pe.wait_ge(x2T_act, 2 * tb + 2)
                            pe.wait_ge(x2T_dve, 2 * tb + 2)
                            if tb in (1, 2):
                                pe.wait_ge(sum_ready, 12 + 2 * tb)
                        else:
                            pe.wait_ge(h_ready, f * 4 - 3 + tb)
                        for w in range(2):
                            for t in range(HT):
                                last = mm(banks[:, 2 * tb + w, :], wbuf[:, par, w * H + t * P:w * H + (t + 1) * P],
                                          x2T[:, t, tb * 512:(tb + 1) * 512], start=t == 0, stop=t == HT - 1)
                        last.then_inc(gate_up_out, 1)

                gated_back(0)
                gated_back(1)
                x2_over(0)
                gated_back(2)
                x2_over(1)
                gate_up(0, 0, (0,), first=True)
                gated_back(3)
                x2_over(2)
                gate_up(0, 0, (1,), first=True)
                x2_over(3)
                gate_up(0, 0, (2, 3), first=True)
                with pe.Fori(1, FT - 1, 2) as f:
                    gate_up(f, 1)
                    gate_up(f + 1, 0)
                pe.wait_ge(wd_ready, FT)
                for t in range(TT):
                    if t < 8:
                        pe.wait_ge(h_ready, FT * 4)
                    else:
                        pe.wait_ge(res_ready, t - 7)
                    for f in range(FT):
                        rows = P if f < FT - 1 else FLAST
                        last = mm(banks[:, t % 8, :], hT[0:rows, f, t * P:(t + 1) * P], wd[0:rows, f, :],
                                  start=f == 0, stop=f == FT - 1)
                    last.then_inc(down_out, 1)

            @block.scalar
            def _(act):
                A = nc.scalar.activation

                def gates(b):
                    act.wait_ge(x1_in[b], 16)
                    if b >= 2:
                        act.wait_ge(gated, b - 1)
                    A(gate[b % 2], x1b[b], ACT.Silu).then_inc(gate_ready, 1)

                def norm_apply(b):
                    act.wait_ge(shift_ready, b + 1)
                    for lt in range(4):
                        A(x1b[b][:, lt, :], x1b[b][:, lt, :], ACT.Identity, bias=shift[:, lt:lt + 1],
                          scale=rstd[:, lt:lt + 1]).then_inc(x2_ready, 1)

                def keep_x2T(b):
                    for ht in range(2):
                        act.wait_ge(x2T_out, b * 4 + ht + 1)
                        A(x2T[:, ht, b * 512:(b + 1) * 512], banks[:, 6 + ht % 2, :], ACT.Copy).then_inc(x2T_act, 1)

                def leaves(f, par, halves=(0, 1), first=False):
                    for c in halves:
                        act.wait_ge(bits_ready, f * 8 + 4 * c + 1)
                        for j in range(8):
                            if j == 0:
                                if not first:
                                    act.wait_ge(gate_up_out, f * 4 - 4)
                                    act.wait_ge(wd_ready, f - 1)
                            else:
                                act.wait_ge(mux_ready, f * 14 + 7 * c + LEAF_AFTER[j])
                            dst = wbuf[:, par, c * HALF:(c + 1) * HALF] if j == 0 else leaf[:, LEAF_BUF[j] - 1, :]
                            A(dst, bits[:, 0, :], ACT.Identity, bias=table[:, 2 * j:2 * j + 1],
                              scale=table_gap[:, j:j + 1]).then_inc(leaf_ready, 1)

                act.wait_ge(gap_ready, 1)
                leaves(0, 0, (0,), first=True)
                gates(0)
                leaves(0, 0, (1,), first=True)
                gates(1)
                for b in range(S):
                    norm_apply(b)
                    if b + 2 < S:
                        gates(b + 2)
                    keep_x2T(b)

                def silus(f):
                    for tb in range(TB):
                        act.wait_ge(gate_up_out, f * 4 + tb + 1)
                        act.wait_ge(h_ready, f * 4 + max(tb - 1, 0) if tb < 2 else f * 4 + tb - 1)
                        A(silu[:, tb % 2, :], banks[:, 2 * tb, :], ACT.Silu).then_inc(silu_ready, 1)

                leaves(1, 1, first=True)
                silus(0)
                with act.Fori(1, FT - 2, 2) as f:
                    leaves(f + 1, 0)
                    silus(f)
                    leaves(f + 2, 1)
                    silus(f + 1)
                leaves(FT - 1, 0)
                silus(FT - 2)
                silus(FT - 1)
                for t in range(TT):
                    act.wait_ge(shift4_ready, t + 1)
                    A(res[:, t % RR, :], res[:, t % RR, :], ACT.Identity, bias=shift[:, t % 4:t % 4 + 1],
                      scale=rstd[:, t % 4:t % 4 + 1]).then_inc(out_ready, 1)

            @block.vector
            def _(dve):
                V = nc.vector

                def gate_y(b):
                    dve.wait_ge(gate_ready, b + 1)
                    dve.wait_ge(y_in[b], 16)
                    V.tensor_tensor(yb[b], yb[b], gate[b % 2], ALU.mult).then_inc(gated, 1)

                def residual(b):
                    for lt in range(4):
                        dve.wait_ge(yT_out, b * 4 + lt + 1)
                        V.tensor_tensor(x1b[b][:, lt, :], banks[:, 2 + lt, :], x1b[b][:, lt, :], ALU.add)\
                            .then_inc(sum_ready, 1)
                    for lt in range(4):
                        dve.wait_ge(sum_ready, b * 4 + lt + 1)
                        V.bn_stats(stats[:, lt, :], x1b[b][:, lt, :]).then_inc(stat_ready, 1)
                    for lt in range(4):
                        dve.wait_ge(stat_ready, b * 4 + lt + 1)
                        V.bn_aggr(meanvar[:, lt, :], stats[:, lt, :]).then_inc(mv_ready, 1)
                    dve.wait_ge(mv_ready, b * 4 + 4)
                    V.tensor_scalar(vareps[:], meanvar[:, :, 1], EPS, None, ALU.add).then_inc(ve_ready, 1)
                    dve.wait_ge(rstd_ready, b + 1)
                    V.scalar_tensor_tensor(shift[:], meanvar[:, :, 0], -1.0, rstd[:], ALU.mult, ALU.mult)\
                        .then_inc(shift_ready, 1)

                def keep_x2T(b):
                    for ht in range(2, 4):
                        dve.wait_ge(x2T_out, b * 4 + ht + 1)
                        V.tensor_copy(x2T[:, ht, b * 512:(b + 1) * 512], banks[:, 6 + ht % 2, :]).then_inc(x2T_dve, 1)

                def decode(f, par):
                    for c in range(2):
                        dve.wait_ge(idx_in, f * 16 + 16)
                        dve.wait_ge(leaf_ready, f * 16 + 8 * c)
                        dve.wait_ge(mux_ready, f * 14 + 7 * c)
                        for k in range(4):
                            V.tensor_scalar(bits[:, k, :], idx_sb[:, par, c * HALF:(c + 1) * HALF], 1 << k, None,
                                            ALU.bitwise_and).then_inc(bits_ready, 1)
                        at = lambda n: wbuf[:, par, c * HALF:(c + 1) * HALF] if n == 0 else leaf[:, n - 1, :]
                        for m, (kept, other, bit) in enumerate(MUX):
                            dve.wait_ge(leaf_ready, f * 16 + 8 * c + MUX_LEAVES[m])
                            dve.wait_ge(bits_ready, f * 8 + 4 * c + 4)
                            if m:
                                dve.wait_ge(mux_ready, f * 14 + 7 * c + m)
                            V.memset(wait_here[:], 0.0)
                            V.copy_predicated(at(kept), bits[:, bit, :], at(other)).then_inc(mux_ready, 1)

                dve.wait_ge(lut_in, 16)
                pairs = table[:].rearrange("p (j two) -> p j two", two=2)
                V.tensor_tensor(table_gap[:], pairs[:, :, 1], pairs[:, :, 0], ALU.subtract).then_inc(gap_ready, 1)
                decode(0, 0)
                gate_y(0)
                gate_y(1)
                for b in range(S):
                    residual(b)
                    if b + 2 < S:
                        gate_y(b + 2)
                    keep_x2T(b)

                def inner(f):
                    for tb in range(TB):
                        dve.wait_ge(silu_ready, f * 4 + tb + 1)
                        V.tensor_tensor(hT[:, f, tb * 512:(tb + 1) * 512], silu[:, tb % 2, :],
                                        banks[:, 2 * tb + 1, :], ALU.mult).then_inc(h_ready, 1)

                decode(1, 1)
                dve.wait_ge(x2_out, 16 * S)
                inner(0)
                with dve.Fori(1, FT - 2, 2) as f:
                    decode(f + 1, 0)
                    inner(f)
                    decode(f + 2, 1)
                    inner(f + 1)
                decode(FT - 1, 0)
                inner(FT - 2)
                inner(FT - 1)

                for t in range(TT):
                    r = res[:, t % RR, :]
                    j = t % 4
                    dve.wait_ge(down_out, t + 1)
                    dve.wait_ge(x2_in, 16 * t + 16)
                    V.tensor_tensor(r, banks[:, t % 8, :], r, ALU.add).then_inc(res_ready, 1)
                    dve.wait_ge(res_ready, t + 1)
                    V.bn_stats(stats[:, j, :], r).then_inc(stat4_ready, 1)
                    dve.wait_ge(stat4_ready, t + 1)
                    V.bn_aggr(meanvar[:, j, :], stats[:, j, :]).then_inc(mv4_ready, 1)
                    dve.wait_ge(mv4_ready, t + 1)
                    V.tensor_scalar(vareps[:, j:j + 1], meanvar[:, j, 1:2], EPS, None, ALU.add)\
                        .then_inc(ve4_ready, 1)
                    dve.wait_ge(rstd4_ready, t + 1)
                    V.scalar_tensor_tensor(shift[:, j:j + 1], meanvar[:, j, 0:1], -1.0, rstd[:, j:j + 1],
                                           ALU.mult, ALU.mult).then_inc(shift4_ready, 1)

            @block.gpsimd
            def _(pool):
                G = nc.gpsimd
                for b in range(S):
                    pool.wait_ge(ve_ready, b + 1)
                    if b:
                        pool.wait_ge(x2_ready, 4 * b)
                    G.tensor_tensor(rstd[:], vareps[:], minus_half[:], ALU.pow).then_inc(rstd_ready, 1)

                def keep_down(f, par):
                    pool.wait_ge(mux_ready, f * 14 + 14)
                    G.tensor_copy(wd[:, f, :], wbuf[:, par, 2 * H:]).then_inc(wd_ready, 1)

                keep_down(0, 0)
                with pool.Fori(1, FT - 1, 2) as f:
                    keep_down(f, 1)
                    keep_down(f + 1, 0)
                for t in range(TT):
                    j = t % 4
                    pool.wait_ge(ve4_ready, t + 1)
                    if t >= 4:
                        pool.wait_ge(out_ready, t - 3)
                    G.tensor_tensor(rstd[:, j:j + 1], vareps[:, j:j + 1], minus_half[:, j:j + 1], ALU.pow)\
                        .then_inc(rstd4_ready, 1)


def kernel(**inputs):
    import numpy as np
    import ml_dtypes
    import concourse.bacc as bacc
    from concourse.bass_utils import run_bass_kernel_spmd

    def arr(name):
        return np.asarray(inputs[name])

    x = arr("x")
    wqkv = arr("L0_attn_weight_qkv").reshape(4, QT + 2, HD, H)
    wp = arr("L0_attn_weight_proj").reshape(H, 4, QT, HD)
    per_channel = np.concatenate([
        arr("L0_xattn_conv_w"), arr("L0_xattn_conv_b")[:, None], arr("L0_xattn_dt_proj_b")[:, None],
        arr("L0_xattn_D")[:, None], arr("L0_xattn_A_log")], axis=1)
    xp = arr("L0_xattn_x_proj_w")

    def tiles(w):
        return np.concatenate([w, w[:FT * P - F]], axis=0).reshape(FT, P, H)

    gate_up = [tiles(arr(n)).transpose(0, 2, 1).reshape(FT, HT, P, P).transpose(0, 2, 1, 3).reshape(FT, P, H)
               for n in ("L0_ffn_gate_idx", "L0_ffn_up_idx")]
    down = tiles(arr("L0_ffn_down_idx").T)

    rows = np.arange(P)
    headsum = np.zeros((P, QT, 32), np.float32)
    for qt in range(QT):
        headsum[rows, qt, 4 * qt + rows // HD] = 1
    spread = np.zeros((P, S * QT, P), np.float32)
    for i in range(S):
        for qt in range(QT):
            spread[32 * i + 4 * qt + rows // HD, i * QT + qt, rows] = 1
    pick = np.tile(np.eye(32), (3, 1)).astype(ml_dtypes.bfloat16)

    arrays = {
        "xT": x.transpose(2, 0, 1).reshape(H, S * L),
        "x": x,
        "ctxT": arr("ctx_1024").transpose(2, 0, 1).reshape(DM, S * L),
        "wqkvT": wqkv.transpose(1, 0, 2, 3).reshape(6 * P, H).T,
        "wpT": wp.transpose(2, 1, 3, 0).reshape(H, H),
        "ipT": arr("L0_xattn_in_proj_w").T,
        "chan": per_channel.reshape(ET, P, -1).transpose(1, 0, 2),
        "xpT": np.concatenate([xp[DR:], xp[:DR]], axis=0).T,
        "dtT": arr("L0_xattn_dt_proj_w").T,
        "lut": arr("L0_ffn_lut").reshape(1, 16),
        "idx": np.concatenate(gate_up + [down], axis=2),
        "ident_c": np.eye(P, dtype=np.float32),
        "headsum_c": headsum,
        "spread_c": spread,
        "pick_c": pick,
    }
    nc = bacc.Bacc("TRN2", target_bir_lowering=False, num_devices=1)
    args = {}
    for name, a in arrays.items():
        a = arrays[name] = np.ascontiguousarray(a)
        args[name] = nc.dram_tensor(f"in_{name}", a.shape, mybir.dt.from_np(a.dtype), kind="ExternalInput").ap()
    out = nc.dram_tensor("out_0", (S, L, H), mybir.dt.float32, kind="ExternalOutput").ap()
    decoder_kernel(nc, out=out, **args)
    r = run_bass_kernel_spmd(nc, [{f"in_{n}": a for n, a in arrays.items()}], core_ids=[0])
    return r.results[0]["out_0"]
```

```python
import concourse.bass as bass
from concourse import mybir
from contextlib import ExitStack

S, L, H = 4, 512, 512
QT, HD = 4, 32
DM, DI, DS, DR, TAPS = 256, 512, 16, 16, 4
P = 128
LQ = L // S
ET = DI // P
HT = H // P
NG = 4
NQ = DS // NG
STEPS = NQ * ET
RING = 4
F = 1376
FT = -(-F // P)
FLAST = F - (FT - 1) * P
EPS = 1e-5
MASKED = -1e30
PRIMED = 1

def decoder_kernel(nc, xT, x, ctxT, wqkvT, wpT, ipT, chan, xpT, dtT, lut, idx, ident_c, headsum_c, spread_c,
                   pick_c, out):
    f32, bf16, i32 = mybir.dt.float32, mybir.dt.bfloat16, mybir.dt.int32
    ALU, ACT, AX = mybir.AluOpType, mybir.ActivationFunctionType, mybir.AxisListType

    x1_scratch = nc.dram_tensor("x1_scratch", [S, L, H], f32, kind="Internal").ap()
    y_scratch = nc.dram_tensor("y_scratch", [S, DI, L], f32, kind="Internal").ap()
    x2_scratch = nc.dram_tensor("x2_scratch", [S, L, H], f32, kind="Internal").ap()

    wd_scratch = nc.dram_tensor("wd_scratch", [FT, P, H], f32, kind="Internal").ap()

    top = ExitStack()
    with top:
        def sem(name, ctx=top):
            return ctx.enter_context(nc.semaphore(name))

        ident = top.enter_context(nc.sbuf_tensor("ident", [P, P], f32))
        banks = top.enter_context(nc.psum_tensor("banks", [P, 8, 512], f32))
        stats = top.enter_context(nc.sbuf_tensor("stats", [P, 4, 6], f32))
        meanvar = top.enter_context(nc.sbuf_tensor("meanvar", [P, 4, 2], f32))
        vareps = top.enter_context(nc.sbuf_tensor("vareps", [P, 4], f32))
        rstd = top.enter_context(nc.sbuf_tensor("rstd", [P, 4], f32))
        shift = top.enter_context(nc.sbuf_tensor("shift", [P, 4], f32))
        minus_half = top.enter_context(nc.sbuf_tensor("minus_half", [P, 4], f32))

        stage1(nc, top, ident, banks, (stats, meanvar, vareps, rstd, shift, minus_half), xT, x, ctxT, wqkvT, wpT,
               ipT, chan, xpT, dtT, ident_c, headsum_c, spread_c, pick_c, x1_scratch, y_scratch)
        stage234(nc, top, ident, banks, (stats, meanvar, vareps, rstd, shift, minus_half), lut, idx,
                 x1_scratch, y_scratch, x2_scratch, wd_scratch, out)


def stage1(nc, top, ident, banks, ln, xT, x, ctxT, wqkvT, wpT, ipT, chan, xpT, dtT, ident_c, headsum_c,
           spread_c, pick_c, x1_scratch, y_scratch):
    f32, bf16 = mybir.dt.float32, mybir.dt.bfloat16
    ALU, ACT, AX = mybir.AluOpType, mybir.ActivationFunctionType, mybir.AxisListType
    stats, meanvar, vareps, rstd, shift, minus_half = ln
    ctx = ExitStack()
    with ctx:
        def sb(name, shape, dt=f32):
            return ctx.enter_context(nc.sbuf_tensor(name, shape, dt))

        def sem(name):
            return ctx.enter_context(nc.semaphore(name))

        wqkv = sb("wqkv", [P, HT, 6 * P])
        wp = sb("wp", [P, QT, H])
        ip = sb("ip", [P, DM // P, DI])
        ch = sb("ch", [P, ET, TAPS + 3 + DS])
        xp_w = sb("xp_w", [P, ET, 3 * DS])
        dt_w = sb("dt_w", [DR, DI])
        headsum = sb("headsum", [P, QT, 32])
        spread = sb("spread", [P, S * QT, P])
        pick = sb("pick", [96, 32], bf16)
        negA = sb("negA", [P, ET, DS])
        ctx_sb = sb("ctx_sb", [P, DM // P, L])
        xT_sb = sb("xT_sb", [P, HT, S, LQ])
        x_sb = sb("x_sb", [P, S, H])
        q = sb("q", [P, QT, S, LQ])
        kv = sb("kv", [P, 2, S, LQ])
        prod_b = sb("prod_b", [P, QT, S - 1, LQ])
        prob = sb("prob", [P, S, LQ])
        rowmax = sb("rowmax", [P, LQ])
        rowsum = sb("rowsum", [P, LQ])
        rowinv = sb("rowinv", [P, LQ])
        conv_in = sb("conv_in", [P, ET, TAPS - 1 + L])
        u = sb("u", [P, ET, L])
        bc_parts = sb("bc_parts", [96, L], bf16)
        bc_rest = sb("bc_rest", [32, L])
        bc_mid = sb("bc_mid", [32, L], bf16)
        dt_lo = sb("dt_lo", [DR, L])
        delta = sb("delta", [P, ET, L])
        du = sb("du", [P, ET, L])
        brep = sb("brep", [P, 2, NG, L])
        crep = sb("crep", [P, 2, NG, L])
        decay = sb("decay", [P, 2, NG, L])
        state = sb("state", [P, RING, NG, L])
        y_sb = sb("y_sb", [P, ET, L])
        conv_w = lambda et, j: ch[:, et, j:j + 1]
        conv_b = lambda et: ch[:, et, TAPS:TAPS + 1]
        dt_b = lambda et: ch[:, et, TAPS + 1:TAPS + 2]
        skip_d = lambda et: ch[:, et, TAPS + 2:TAPS + 3]
        a_log = ch[:, :, TAPS + 3:TAPS + 3 + DS]
        k, v = kv[:, 0], kv[:, 1]
        conv_acc, expneg, relu = state[:, 0], state[:, 1], state[:, 2]
        prod = [prod_b[:, :, 0:1, :], prod_b[:, :, 1:3, :],
                crep[:, 1].rearrange("p t (s l) -> p t s l", s=S)[:, :, 0:3, :],
                brep[:, 1].rearrange("p t (s l) -> p t s l", s=S)]
        flat_prod = prod_b[:].rearrange("p t s l -> p (t s l)")
        pv = [flat_prod[:, 0:512], flat_prod[:, 512:1024]]

        (ip_in, ch_in, wqkv_in, w_in, ctx_in, xT_in, x_in, negA_ready, setup_done, inproj_out, qkv_out, xproj_out,
         delta_out, score_out, rep_out, pb_out, proj_out, nsum_done, xp_ready, qkv_ready, conv_tap, u_ready,
         bc_hi, bc_r1, bc_m, bc_lo, dtlo_ready, abs_ready, expneg_ready, onep_ready, ln_ready, corr_ready,
         base_ready, relu_ready, delta_ready, du_ready, prod_ready, masked, max_ready, sub_ready, exp_ready,
         sum_ready, inv_ready, prob_ready, pv_mul, pv_sum, rep_ready, decay_ready, dbu_ready, scan_ready,
         hc_ready, res_ready, stat_ready, mv_ready, ve_ready, rstd_ready, shift_ready, x1_ready, x1_out,
         y_ready, y_out, half_ready, dbu_pool, du0_ready) = [sem(n) for n in (
             "ip_in ch_in wqkv_in w_in ctx_in xT_in x_in negA_ready setup_done inproj_out qkv_out xproj_out "
             "delta_out score_out rep_out pb_out proj_out nsum_done xp_ready qkv_ready conv_tap u_ready "
             "bc_hi bc_r1 bc_m bc_lo dtlo_ready abs_ready expneg_ready onep_ready ln_ready corr_ready "
             "base_ready relu_ready delta_ready du_ready prod_ready masked max_ready sub_ready exp_ready "
             "sum_ready inv_ready prob_ready pv_mul pv_sum rep_ready decay_ready dbu_ready scan_ready "
             "hc_ready res_ready stat_ready mv_ready ve_ready rstd_ready shift_ready x1_ready x1_out "
             "y_ready y_out half_ready dbu_pool du0_ready").split()]
        SEQ = [4, 0, 1, 2, 3, 5]
        SEQ_BANK = [4, 5, 6, 4, 5, 4]
        SEQ_AFTER = {3: 1, 4: 2, 5: 4}
        BY_POOL = (3, 7)
        POOL_AT = {t - 2 if t > RING else 0: t for t in BY_POOL}
        pool_before = lambda t: sum(n < t for n in BY_POOL)
        N_DBU = STEPS - len(BY_POOL)
        N_W = 7
        TILES = [S // (i + 1) for i in range(S)]
        ITEMS = [(i, qt, TILES[i]) for i in range(S) for qt in range(0, QT, TILES[i])]
        N_IT = len(ITEMS)
        UPTO = [sum(i <= s for i, _, _ in ITEMS) for s in range(S)]
        AT = {2: [("p", 0), ("p", 1)], 3: [("p", 2), ("p", 3)], 4: [("p", 4), ("p", 5)],
              5: [("p", 6), ("p", 7)], 6: [("p", 8), ("p", 9)], 7: [("p", 10)],
              8: [("out", 0)], 9: [("out", 1)], 10: [("out", 2)], 12: [("out", 3)]}
        LAG = 2
        TURNS = [w for t in sorted(AT) for w in AT[t]]

        with nc.Block() as block:

            @block.sync
            def _(sp):
                sp.dma_start(ip[:], ipT.rearrange("(t p) n -> p t n", p=P)).then_inc(ip_in, 16)

                def load(b, first=False):
                    if not first:
                        sp.wait_ge(inproj_out, b * ET)
                    sp.dma_start(ctx_sb[:], ctxT.rearrange("(t p) (b l) -> p t b l", p=P, b=S)[:, :, b, :])\
                        .then_inc(ctx_in, 16)
                    if not first:
                        sp.wait_ge(qkv_out, b * 6)
                    for t in range(HT):
                        source = xT.rearrange("(t p) (s c l) -> t p s c l", p=P, s=S, c=S)[t, :, :, b, :]
                        sp.dma_start(xT_sb[:, t], source)\
                            .then_inc(xT_in, 16)
                    if not first:
                        sp.wait_ge(x1_out, b * 16)
                    sp.dma_start(x_sb[:], x.rearrange("s (c p) h -> p s c h", p=P)[:, :, b, :]).then_inc(x_in, 16)

                load(0, first=True)
                with sp.Fori(1, S) as b:
                    load(b)


            @block.tensor
            def _(pe):
                mm = nc.tensor.matmul
                pe.sem_inc(nsum_done, PRIMED)
                pe.wait_ge(ip_in, 16)
                with pe.Fori(0, S) as b:
                    pe.wait_ge(ctx_in, b * 16 + 16)
                    pe.wait_ge(res_ready, PRIMED + b * S)
                    pe.wait_ge(rep_ready, PRIMED + b * 2 * DS)
                    for et in range(ET):
                        for t in range(DM // P):
                            last = mm(banks[:, et, :], ip[:, t, et * P:(et + 1) * P], ctx_sb[:, t, :],
                                      start=t == 0, stop=t == DM // P - 1)
                        last.then_inc(inproj_out, 1)

                    def qkv(n):
                        m = SEQ[n]
                        if n in SEQ_AFTER:
                            pe.wait_ge(qkv_ready, b * 6 + SEQ_AFTER[n])
                        for t in range(HT):
                            last = mm(banks[:, SEQ_BANK[n], :], wqkv[:, t, m * P:(m + 1) * P],
                                      xT_sb[:, t].rearrange("p s l -> p (s l)"), start=t == 0, stop=t == HT - 1)
                        last.then_inc(qkv_out, 1)

                    pe.wait_ge(wqkv_in, 16)
                    pe.wait_ge(xT_in, b * 64 + 64)
                    pe.wait_ge(y_ready, PRIMED + b * ET)
                    qkv(0)
                    qkv(1)
                    qkv(2)
                    pe.wait_ge(w_in, N_W * 16)
                    pe.wait_ge(xp_ready, b * ET + 4)
                    for et in range(ET):
                        pe.wait_ge(u_ready, b * ET + et + 1)
                        last = mm(banks[0:2 * DS + DR, 0, :], xp_w[:, et, :], u[:, et, :],
                                  start=et == 0, stop=et == ET - 1)
                    last.then_inc(xproj_out, 1)
                    pe.wait_ge(dtlo_ready, b + 1)
                    for et in (1, 2, 3, 0):
                        if et == 0:
                            pe.wait_ge(bc_r1, b + 1)
                        mm(banks[:, et, :], dt_w[:, et * P:(et + 1) * P], dt_lo[:],
                           start=True, stop=True).then_inc(delta_out, 1)
                    qkv(3)

                    def repeat_rows(g, rs):
                        for r in rs:
                            if g == 0:
                                bank = 6 + r % 2
                                if r == 0:
                                    pe.wait_ge(qkv_ready, b * 6 + 3)
                            else:
                                bank = 2 + r % 2
                                if g == 1 and r < 2:
                                    pe.wait_ge(relu_ready, b * ET + ET)
                            if g or r >= 2:
                                pe.wait_ge(rep_ready, PRIMED + b * 2 * DS + 2 * NG * g + r - 1)
                            row = (DS if r >= NG else 0) + NG * g + r % NG
                            mm(banks[:, bank, :], pick[:, row:row + 1].to_broadcast([96, P]), bc_parts[:],
                               start=True, stop=True).then_inc(rep_out, 1)

                    pe.wait_ge(bc_lo, b + 1)
                    pe.wait_ge(bc_m, b * 2 + 2)
                    repeat_rows(0, (0, 1))
                    qkv(4)
                    repeat_rows(0, (2, 3))
                    qkv(5)
                    repeat_rows(0, (4, 5))
                    pe.wait_ge(relu_ready, b * ET + ET)
                    pe.wait_ge(prod_ready, b * 16 + 16)
                    for i in range(S):
                        for qt in range(QT):
                            last = mm(banks[32 * i:32 * i + 32, 0, 0:(i + 1) * LQ], headsum[:, qt, :],
                                      prod[i][:, qt].rearrange("p j l -> p (j l)"),
                                      start=qt == 0, stop=qt == QT - 1)
                        last.then_inc(score_out, 1)
                    repeat_rows(0, (6, 7))

                    def wait_for_bank(what):
                        turn = TURNS.index(what)
                        if turn >= 2:
                            kind, n = TURNS[turn - 2]
                            if kind == "p":
                                pe.wait_ge(pv_mul, b * N_IT + n + 1)
                            else:
                                pe.wait_ge(res_ready, PRIMED + b * S + n + 1)
                        return turn % 2

                    def repeat_probs(n):
                        i, qt0, tiles = ITEMS[n]
                        if n == 0:
                            pe.wait_ge(prob_ready, b + 1)
                        bank = wait_for_bank(("p", n))
                        for c in range(tiles):
                            last = mm(banks[:, bank, c * (i + 1) * LQ:(c + 1) * (i + 1) * LQ],
                                      spread[:, i * QT + qt0 + c, :],
                                      prob[:, 0:i + 1, :].rearrange("p j l -> p (j l)"), start=True, stop=True)
                        last.then_inc(pb_out, 1)

                    def project(s):
                        pe.wait_ge(pv_sum, PRIMED + b * N_IT + UPTO[s])
                        bank = wait_for_bank(("out", s))
                        for qt in range(QT):
                            last = mm(banks[:, bank, :], q[:, qt, s, :], wp[:, qt, :],
                                      start=qt == 0, stop=qt == QT - 1)
                        last.then_inc(proj_out, 1)

                    for t in range(STEPS):
                        g, et = t // ET, t % ET
                        if g < NQ - 1 and (t == 0 or et < 3 and t > 0):
                            if t == 0:
                                repeat_rows(1, (0, 1))
                            repeat_rows(g + 1, (2 * et + 2, 2 * et + 3))
                        if et == 3 and g + 2 < NQ:
                            repeat_rows(g + 2, (0, 1))
                        for kind, n in AT.get(t, ()):
                            (repeat_probs if kind == "p" else project)(n)
                        if t == 0:
                            pe.wait_ge(qkv_ready, b * 6 + 6)
                            pe.wait_ge(rep_ready, PRIMED + b * 2 * DS + 2 * NG)
                        pe.wait_ge(hc_ready, PRIMED + b * STEPS + t + 1)
                        for n in range(NG):
                            last = mm(banks[:, 4 + et, :], ident[:], state[:, t % RING, n, :],
                                      start=(g == 0 and n == 0), stop=(g == NQ - 1 and n == NG - 1))
                        last.then_inc(nsum_done, 1)

            @block.scalar
            def _(act):
                A = nc.scalar.activation
                act.dma_start(ch[:], chan).then_inc(ch_in, 16)
                act.dma_start(wqkv[:], wqkvT.rearrange("(t p) n -> p t n", p=P)).then_inc(wqkv_in, 16)
                act.dma_start(xp_w[:], xpT.rearrange("(t p) n -> p t n", p=P)).then_inc(w_in, 16)
                act.dma_start(dt_w[:], dtT).then_inc(w_in, 16)
                act.dma_start(pick[:], pick_c).then_inc(w_in, 16)
                act.dma_start(headsum[:], headsum_c).then_inc(w_in, 16)
                act.dma_start(spread[:], spread_c).then_inc(w_in, 16)
                act.dma_start(wp[:], wpT.rearrange("(t p) n -> p t n", p=P)).then_inc(w_in, 16)
                act.dma_start(ident[:], ident_c).then_inc(w_in, 16)
                act.wait_ge(ch_in, 16)
                A(negA[:], a_log, ACT.Exp).then_inc(negA_ready, 1)
                act.sem_inc(rep_ready, PRIMED)
                act.wait_ge(setup_done, 4)
                with act.Fori(0, S) as b:
                    act.wait_ge(conv_tap, PRIMED + b * 16)
                    for et in range(ET):
                        act.wait_ge(inproj_out, b * ET + et + 1)
                        A(conv_in[:, et, TAPS - 1:], banks[:, et, :], ACT.Copy).then_inc(xp_ready, 1)

                    def keep_qkv(n):
                        m = SEQ[n]
                        act.wait_ge(qkv_out, b * 6 + n + 1)
                        dst = q[:, m] if m < QT else kv[:, m - QT]
                        A(dst.rearrange("p s l -> p (s l)"), banks[:, SEQ_BANK[n], :], ACT.Copy).then_inc(qkv_ready, 1)

                    act.wait_ge(pv_sum, PRIMED + b * N_IT)
                    act.wait_ge(res_ready, PRIMED + b * S)
                    act.wait_ge(y_ready, PRIMED + b * ET)
                    keep_qkv(0)
                    for et in range(ET):
                        act.wait_ge(conv_tap, PRIMED + b * 16 + 12 + et + 1)
                        A(u[:, et, :], conv_acc[:, et, :], ACT.Silu).then_inc(u_ready, 1)
                    keep_qkv(1)
                    keep_qkv(2)
                    act.wait_ge(xproj_out, b + 1)
                    A(dt_lo[:], banks[2 * DS:2 * DS + DR, 0, :], ACT.Copy).then_inc(dtlo_ready, 1)
                    A(bc_parts[0:32, :], banks[0:32, 0, :], ACT.Copy).then_inc(bc_hi, 1)
                    act.wait_ge(nsum_done, PRIMED + b * STEPS)
                    for n, et in enumerate((1, 2, 3, 0)):
                        if et == 0:
                            act.wait_ge(bc_r1, b + 1)
                            A(bc_mid[:], bc_rest[:], ACT.Copy).then_inc(bc_m, 1)
                            A(bc_parts[32:64, :], bc_rest[:], ACT.Copy).then_inc(bc_m, 1)
                        act.wait_ge(delta_out, b * ET + n + 1)
                        A(expneg[:, et, :], banks[:, et, :], ACT.Abs, bias=dt_b(et)).then_inc(abs_ready, 1)
                    act.wait_ge(abs_ready, b * ET + ET)
                    A(expneg[:], expneg[:], ACT.Exp, scale=-1.0).then_inc(expneg_ready, 1)
                    def keep_rows(g, rs):
                        for r in rs:
                            act.wait_ge(rep_out, b * 2 * DS + 2 * NG * g + r + 1)
                            dst = brep if r < NG else crep
                            bank = 6 + r % 2 if g == 0 else 2 + r % 2
                            A(dst[:, g % 2, r % NG, :], banks[:, bank, :], ACT.Copy).then_inc(rep_ready, 1)

                    act.wait_ge(dbu_ready, PRIMED + b * N_DBU)
                    act.wait_ge(hc_ready, PRIMED + b * STEPS)
                    keep_qkv(3)
                    keep_rows(0, (0, 1))
                    act.wait_ge(onep_ready, b + 1)
                    A(delta[:], conv_acc[:], ACT.Ln).then_inc(ln_ready, 1)
                    keep_qkv(4)
                    keep_rows(0, (2, 3))
                    for t in range(STEPS):
                        g, et = t // ET, t % ET
                        act.wait_ge(scan_ready, PRIMED + b * STEPS + max(t - 1, 0))
                        act.wait_ge(delta_ready, b * ET + min(t, ET - 1) + 1)
                        for n in range(NG):
                            A(decay[:, t % 2, n, 1:], delta[:, et, 1:], ACT.Exp,
                              scale=negA[:, et, NG * g + n:NG * g + n + 1]).then_inc(decay_ready, 1)
                        if t == 0:
                            keep_qkv(5)
                            keep_rows(0, range(4, 8))
                        if t == 2:
                            act.wait_ge(score_out, b * S + S)
                        if et in (2, 3) and g < NQ - 1:
                            keep_rows(g + 1, range(2 * (et - 2), 2 * (et - 1)))
                        if et in (0, 1) and g:
                            act.wait_ge(hc_ready, PRIMED + b * STEPS + ET * (g - 1))
                            keep_rows(g, range(4 + 2 * et, 6 + 2 * et))
                        if t == 2:
                            act.wait_ge(sub_ready, b + 1)
                            A(prob[:], prob[:], ACT.Exp, scale=float(HD) ** -0.5).then_inc(exp_ready, 1)

            @block.vector
            def _(dve):
                V = nc.vector
                V.memset(decay[:, :, :, 0:1], 0.0).then_inc(setup_done, 1)
                V.memset(conv_in[:, :, 0:TAPS - 1], 0.0).then_inc(setup_done, 1)
                V.memset(prob[:], 0.0).then_inc(setup_done, 1)
                dve.wait_ge(negA_ready, 1)
                V.tensor_scalar(negA[:], negA[:], -1.0, None, ALU.mult).then_inc(setup_done, 1)
                for primed in (res_ready, y_ready, conv_tap, pv_sum, dbu_ready, scan_ready):
                    dve.sem_inc(primed, PRIMED)
                with dve.Fori(0, S) as b:
                    dve.wait_ge(nsum_done, PRIMED + b * STEPS)
                    for j in range(TAPS):
                        for et in range(ET):
                            tap = conv_in[:, et, j:j + L]
                            if j == 0:
                                dve.wait_ge(xp_ready, b * ET + et + 1)
                                V.tensor_scalar(conv_acc[:, et, :], tap, conv_w(et, 0), conv_b(et), ALU.mult,
                                                ALU.add).then_inc(conv_tap, 1)
                            else:
                                dve.wait_ge(conv_tap, PRIMED + b * 16 + 4 * (j - 1) + et + 1)
                                V.scalar_tensor_tensor(conv_acc[:, et, :], tap, conv_w(et, j), conv_acc[:, et, :],
                                                       ALU.mult, ALU.add).then_inc(conv_tap, 1)

                    dve.wait_ge(bc_hi, b + 1)
                    V.tensor_tensor(bc_rest[:], banks[0:32, 0, :], bc_parts[0:32, :], ALU.subtract).then_inc(bc_r1, 1)
                    for n, et in enumerate((1, 2, 3, 0)):
                        dve.wait_ge(abs_ready, b * ET + n + 1)
                        V.tensor_scalar(relu[:, et, :], banks[:, et, :], dt_b(et), 0.0, ALU.add, ALU.max)\
                            .then_inc(relu_ready, 1)
                    dve.wait_ge(bc_r1, b + 1)
                    dve.wait_ge(bc_m, b * 2 + 1)
                    V.tensor_tensor(bc_parts[64:96, :], bc_rest[:], bc_mid[:], ALU.subtract).then_inc(bc_lo, 1)
                    dve.wait_ge(expneg_ready, b + 1)
                    V.tensor_scalar(conv_acc[:], expneg[:], 1.0, None, ALU.add).then_inc(onep_ready, 1)
                    dve.wait_ge(onep_ready, b + 1)
                    V.scalar_tensor_tensor(expneg[:], conv_acc[:], -1.0, expneg[:], ALU.add, ALU.subtract)\
                        .then_inc(corr_ready, 1)
                    dve.wait_ge(corr_ready, b + 1)
                    dve.wait_ge(relu_ready, b * ET + ET)
                    V.tensor_tensor(relu[:], relu[:], expneg[:], ALU.subtract).then_inc(base_ready, 1)
                    dve.wait_ge(base_ready, b + 1)
                    dve.wait_ge(ln_ready, b + 1)
                    for et in range(ET):
                        V.tensor_tensor(delta[:, et, :], delta[:, et, :], relu[:, et, :], ALU.add)\
                            .then_inc(delta_ready, 1)
                        if et == 1:
                            dve.wait_ge(delta_ready, b * ET + 1)
                            V.tensor_tensor(du[:, 0, :], delta[:, 0, :], u[:, 0, :], ALU.mult).then_inc(du0_ready, 1)

                    def softmax_difference():
                        dve.wait_ge(score_out, b * S + S)
                        for i in range(S - 1):
                            V.memset(banks[32 * i:32 * i + 32, 0, (i + 1) * LQ:], MASKED).then_inc(masked, 1)
                        dve.wait_ge(masked, b * 3 + 3)
                        sc = banks[:, 0, :].rearrange("p (j l) -> p j l", j=S)
                        V.tensor_reduce(rowmax[:], sc.rearrange("p j l -> p l j"), AX.X, ALU.max).then_inc(max_ready, 1)
                        dve.wait_ge(max_ready, b + 1)
                        V.tensor_tensor(prob[:], sc, rowmax[:].unsqueeze(1).to_broadcast([P, S, LQ]), ALU.subtract)\
                            .then_inc(sub_ready, 1)

                    def softmax_quotient():
                        dve.wait_ge(exp_ready, b + 1)
                        V.tensor_reduce(rowsum[:], prob[:].rearrange("p j l -> p l j"), AX.X, ALU.add)\
                            .then_inc(sum_ready, 1)
                        dve.wait_ge(sum_ready, b + 1)
                        V.reciprocal(rowinv[:], rowsum[:]).then_inc(inv_ready, 1)
                        dve.wait_ge(inv_ready, b + 1)
                        V.tensor_tensor(prob[:], prob[:], rowinv[:].unsqueeze(1).to_broadcast([P, S, LQ]), ALU.mult)\
                            .then_inc(prob_ready, 1)

                    def pv_product(n):
                        i, qt0, tiles = ITEMS[n]
                        dve.wait_ge(pb_out, b * N_IT + n + 1)
                        if n == 0:
                            dve.wait_ge(qkv_ready, b * 6 + 6)
                        if n >= 2:
                            dve.wait_ge(pv_sum, PRIMED + b * N_IT + n - 1)
                        shape = [P, tiles, i + 1, LQ]
                        size = tiles * (i + 1) * LQ
                        repeated = banks[:, TURNS.index(("p", n)) % 2, 0:size]
                        V.tensor_tensor(pv[n % 2][:, 0:size].rearrange("p (c j l) -> p c j l", c=tiles, l=LQ),
                                        repeated.rearrange("p (c j l) -> p c j l", c=tiles, l=LQ),
                                        v[:, 0:i + 1, :].unsqueeze(1).to_broadcast(shape), ALU.mult)\
                            .then_inc(pv_mul, 1)

                    def pv_total(n):
                        i, qt0, tiles = ITEMS[n]
                        size = tiles * (i + 1) * LQ
                        dve.wait_ge(pv_mul, b * N_IT + n + 1)
                        V.tensor_reduce(q[:, qt0:qt0 + tiles, i, :],
                                        pv[n % 2][:, 0:size].rearrange("p (c j l) -> p c l j", c=tiles, l=LQ),
                                        AX.X, ALU.add).then_inc(pv_sum, 1)

                    def residual(s):
                        dve.wait_ge(proj_out, b * S + s + 1)
                        if s == 0:
                            dve.wait_ge(x_in, b * 16 + 16)
                        projected = banks[:, TURNS.index(("out", s)) % 2, :]
                        V.tensor_tensor(x_sb[:, s, :], projected, x_sb[:, s, :], ALU.add)\
                            .then_inc(res_ready, 1)
                        dve.wait_ge(res_ready, PRIMED + b * S + s + 1)
                        V.bn_stats(stats[:, s, :], x_sb[:, s, :]).then_inc(stat_ready, 1)
                        dve.wait_ge(setup_done, 4)
                        dve.wait_ge(stat_ready, b * S + s + 1)
                        V.bn_aggr(meanvar[:, s, :], stats[:, s, :]).then_inc(mv_ready, 1)

                    def input_product(t):
                        g, et = t // ET, t % ET
                        if t >= RING:
                            dve.wait_ge(nsum_done, PRIMED + b * STEPS + t - RING + 1)
                        dve.wait_ge(rep_ready, PRIMED + b * 2 * DS + 2 * NG * g + NG)
                        if t == 0:
                            dve.wait_ge(du0_ready, b + 1)
                        else:
                            dve.wait_ge(du_ready, b * (ET - 1) + min(t, ET - 1))
                        V.tensor_tensor(state[:, t % RING], du[:, et:et + 1, :].to_broadcast([P, NG, L]),
                                        brep[:, g % 2], ALU.mult).then_inc(dbu_ready, 1)

                    def scan(t):
                        if t in BY_POOL:
                            dve.wait_ge(dbu_pool, b * len(BY_POOL) + pool_before(t) + 1)
                        else:
                            dve.wait_ge(dbu_ready, PRIMED + b * N_DBU + t - pool_before(t) + 1)
                        dve.wait_ge(decay_ready, b * STEPS * NG + NG * t + NG)
                        flat = state[:, t % RING].rearrange("p n l -> p (n l)")
                        V.tensor_tensor_scan(flat, decay[:, t % 2].rearrange("p n l -> p (n l)"), flat, 0.0,
                                             ALU.mult, ALU.add).then_inc(scan_ready, 1)

                    input_product(0)
                    for t in range(STEPS):
                        if t + 1 < STEPS and t + 1 not in BY_POOL:
                            input_product(t + 1)
                        scan(t)
                        if t == 0:
                            softmax_difference()
                        if t == 2:
                            softmax_quotient()
                        for kind, n in AT.get(t - LAG, ()):
                            (pv_product if kind == "p" else residual)(n)
                        for kind, n in AT.get(t - LAG, ()):
                            if kind == "p":
                                pv_total(n)
                    dve.wait_ge(mv_ready, b * S + S)
                    V.tensor_scalar(vareps[:], meanvar[:, :, 1], EPS, None, ALU.add).then_inc(ve_ready, 1)
                    for et in range(ET):
                        dve.wait_ge(nsum_done, PRIMED + b * STEPS + STEPS - ET + et + 1)
                        V.scalar_tensor_tensor(y_sb[:, et, :], u[:, et, :], skip_d(et), banks[:, 4 + et, :],
                                               ALU.mult, ALU.add).then_inc(y_ready, 1)
                    dve.wait_ge(rstd_ready, b + 1)
                    V.scalar_tensor_tensor(shift[:], meanvar[:, :, 0], -1.0, rstd[:], ALU.mult, ALU.mult)\
                        .then_inc(shift_ready, 1)
                    dve.wait_ge(shift_ready, b + 1)
                    for s in range(S):
                        V.tensor_scalar(x_sb[:, s, :], x_sb[:, s, :], rstd[:, s:s + 1], shift[:, s:s + 1],
                                        ALU.mult, ALU.add).then_inc(x1_ready, 1)

            @block.gpsimd
            def _(pool):
                G = nc.gpsimd
                G.memset(minus_half[:], -0.5).then_inc(half_ready, 1)
                pool.wait_ge(half_ready, 1)
                pool.sem_inc(hc_ready, PRIMED)
                with pool.Fori(0, S) as b:
                    for qt in range(QT):
                        pool.wait_ge(qkv_ready, b * 6 + qt + 2)
                        for i in range(S):
                            shape = [P, i + 1, LQ]
                            G.tensor_tensor(prod[i][:, qt], q[:, qt, i:i + 1, :].to_broadcast(shape),
                                            k[:, 0:i + 1, :], ALU.mult).then_inc(prod_ready, 1)
                    for et in range(1, ET):
                        pool.wait_ge(delta_ready, b * ET + et + 1)
                        G.tensor_tensor(du[:, et, :], delta[:, et, :], u[:, et, :], ALU.mult).then_inc(du_ready, 1)

                    def input_product(t):
                        g, et = t // ET, t % ET
                        pool.wait_ge(nsum_done, PRIMED + b * STEPS + max(t - RING + 1, 0))
                        pool.wait_ge(rep_ready, PRIMED + b * 2 * DS + 2 * NG * g + NG)
                        pool.wait_ge(du_ready, b * (ET - 1) + ET - 1)
                        G.tensor_tensor(state[:, t % RING], du[:, et:et + 1, :].to_broadcast([P, NG, L]),
                                        brep[:, g % 2], ALU.mult).then_inc(dbu_pool, 1)

                    for t in range(STEPS):
                        g = t // ET
                        if t in POOL_AT:
                            input_product(POOL_AT[t])
                        pool.wait_ge(rep_ready, PRIMED + b * 2 * DS + 2 * NG * (g + 1))
                        pool.wait_ge(scan_ready, PRIMED + b * STEPS + t + 1)
                        G.tensor_tensor(state[:, t % RING], state[:, t % RING], crep[:, g % 2], ALU.mult)\
                            .then_inc(hc_ready, 1)
                    pool.wait_ge(ve_ready, b + 1)
                    G.tensor_tensor(rstd[:], vareps[:], minus_half[:], ALU.pow).then_inc(rstd_ready, 1)
                    pool.wait_ge(y_ready, PRIMED + b * ET + ET)
                    pool.dma_start(y_scratch.rearrange("b (t p) l -> p b t l", p=P)[:, b], y_sb[:])\
                        .then_inc(y_out, 16)
                    pool.wait_ge(x1_ready, b * S + S)
                    pool.dma_start(x1_scratch.rearrange("s (c p) h -> p s c h", p=P)[:, :, b, :], x_sb[:])\
                        .then_inc(x1_out, 16)
                    pool.wait_ge(y_out, b * 16 + 16)
                pool.wait_ge(x1_out, 16 * S)


def stage234(nc, top, ident, banks, ln, lut, idx, x1_scratch, y_scratch, x2_scratch, wd_scratch, out):
    f32, f32r, i32 = mybir.dt.float32, mybir.dt.float32r, mybir.dt.int32
    ALU, ACT, AX = mybir.AluOpType, mybir.ActivationFunctionType, mybir.AxisListType
    stats, meanvar, vareps, rstd, shift, minus_half = ln
    ctx = ExitStack()
    with ctx:
        def sb(name, shape, dt=f32):
            return ctx.enter_context(nc.sbuf_tensor(name, shape, dt))

        def sem(name):
            return ctx.enter_context(nc.semaphore(name))

        table = sb("table", [P, 16])
        table_gap = sb("table_gap", [P, 8])
        x2T = sb("x2T", [P, 2, HT, S * L], f32r)
        hT = sb("hT", [P, FT, S * L])
        idx_sb = sb("idx_sb", [P, 3, H], i32)
        bit0 = sb("bit0", [P, 2, H], i32)
        bits = sb("bits", [P, 3, H], i32)
        leaf = sb("leaf", [P, 4, H])
        w32 = sb("w32", [P, 3, H])
        wgu = sb("wgu", [P, 2, 2, 2, H], f32r)
        silu = sb("silu", [P, 2, 512])
        wait_here = sb("wait_here", [P, 7])
        pool_wait_here = sb("pool_wait_here", [P, 2])
        flat_h = hT[:].rearrange("p f n -> p (f n)")
        x1b = [flat_h[:, b * 2048:(b + 1) * 2048].rearrange("p (t h) -> p t h", h=H) for b in range(S)]
        yb = [flat_h[:, (4 + b) * 2048:(5 + b) * 2048].rearrange("p (t h) -> p t h", h=L) for b in range(S)]
        gate = [flat_h[:, (8 + b) * 2048:(9 + b) * 2048].rearrange("p (t h) -> p t h", h=H) for b in range(2)]
        flat_x2T = x2T[:].rearrange("p s t n -> p (s t n)")
        WD, HG, HTILE = FT * H, 512, FT * P
        wd = [flat_x2T[:, s * WD:(s + 1) * WD].rearrange("p (f n) -> p f n", n=H) for s in range(2)]
        hg = [[flat_x2T[:, 2 * WD + (2 * r + s) * HG:2 * WD + (2 * r + s + 1) * HG] for s in range(2)]
              for r in range(2)]
        flat_wgu = wgu[:].rearrange("p a b c n -> p (a b c n)")
        at_lo = 2 * WD + 4 * HG
        h_hi = [flat_wgu[:, r * HTILE:(r + 1) * HTILE].rearrange("p (f n) -> p f n", n=P) for r in range(2)]
        h_lo = [flat_x2T[:, at_lo + r * HTILE:at_lo + (r + 1) * HTILE].rearrange("p (f n) -> p f n", n=P)
                for r in range(2)]
        res = leaf

        x1_in = [sem(f"x1_in{b}") for b in range(S)]
        y_in = [sem(f"y_in{b}") for b in range(S)]
        idx_in = [sem(f"idx_in{c}") for c in range(3)]
        wd_in = [sem(f"wd_in{r}") for r in range(3)]
        (gate_ready, gated, sum_out, stat_ready, mv_ready, ve_ready, rstd_ready,
         shift_ready, x2_ready, x2_out, x2T_out, x2hi_ready, x2lo_ready, lut_in, gap_ready, bits_ready,
         top_ready, leaf_ready, leaf7_ready, mux_ready, whi_ready, wlo_ready, wd_stored, gate_up_out, silu_ready,
         h_ready, wdhi_ready, wdlo_ready, hghi_ready, hglo_ready, group_step, hhi_ready, hlo_ready, down_out, x2_in,
         res_ready, stat4_ready, mv4_ready, ve4_ready, rstd4_ready, shift4_ready, out_ready, stored) = [
             sem(n) for n in (
                 "gate_ready gated sum_out stat2_ready mv2_ready ve2_ready rstd2_ready "
                 "shift2_ready x2_ready x2_out x2T_out x2hi_ready x2lo_ready lut_in gap_ready bits_ready "
                 "top_ready leaf_ready leaf7_ready mux_ready whi_ready wlo_ready wd_stored gate_up_out silu_ready "
                 "h_ready wdhi_ready wdlo_ready hghi_ready hglo_ready group_step hhi_ready hlo_ready down_out x2_in "
                 "res4_ready stat4_ready mv4_ready ve4_ready rstd4_ready shift4_ready out_ready stored").split()]
        TT = S * L // P
        GT = 4
        TB = S * L // 512
        RR = 4

        LEAF_ROLE = [0, 1, 2, 3, 1, 3, 2, 4]
        MUX = [(0, 1, 1), (2, 3, 1), (0, 2, 2), (1, 3, 1), (2, 4, 1), (1, 2, 2), (0, 1, 3)]
        MUX_LEAVES = [2, 4, 4, 6, 7, 7, 7]
        MUX_AFTER = {2: 2, 5: 5, 6: 6}
        LEAF_AFTER = {4: 1, 5: 2, 6: 3}
        LEAF_AFTER_LAST = {1: 5, 2: 4, 3: 6}
        ROLES = [(None, 0, 1, 3, 2), (None, 2, 3, 1, 0)]

        def buffer(role, c, parity):
            return leaf[:, ROLES[parity][role], :] if role else w32[:, c, :]

        def X2T_BANK(b, ht):
            return (6 + ht) % 8 if b < 3 else 6 + ht % 2

        ORDER = [("split", 4), ("split", 5), ("norm", 0), ("norm", 1), ("split", 6), ("norm", 2), ("norm", 3),
                 ("norm", 4)]
        for t in range(7, TT):
            ORDER += [("split", t), ("norm", t - 2)]
        ORDER += [("norm", TT - 2), ("norm", TT - 1)]

        with nc.Block() as block:

            @block.sync
            def _(sp):
                def load_idx(f, c):
                    sp.dma_start(idx_sb[:, c, :], idx[f, :, c * H:(c + 1) * H]).then_inc(idx_in[c], 16)

                def next_idx(f, c):
                    sp.wait_ge(mux_ready, f * 21 + 7 * c + 7)
                    load_idx(f + 1, c)

                def store_x2(b):
                    sp.wait_ge(x2_ready, b * 4 + 4)
                    sp.dma_start(x2_scratch[b].rearrange("(t p) h -> p t h", p=P), x1b[b]).then_inc(x2_out, 16)

                def store_wd(f):
                    sp.wait_ge(mux_ready, f * 21 + 21)
                    sp.dma_start(wd_scratch[f], w32[:, 2, :]).then_inc(wd_stored, 16)

                sp.dma_start(table[:], lut.to_broadcast([P, 16])).then_inc(lut_in, 16)
                load_idx(0, 0)
                for b in range(S):
                    sp.dma_start(x1b[b], x1_scratch[b].rearrange("(t p) h -> p t h", p=P)).then_inc(x1_in[b], 16)
                    sp.dma_start(yb[b], y_scratch[b].rearrange("(t p) l -> p t l", p=P)).then_inc(y_in[b], 16)
                    if b in (0, 1):
                        load_idx(0, b + 1)
                next_idx(0, 0)
                next_idx(0, 1)
                store_x2(0)
                next_idx(0, 2)
                store_x2(1)
                store_wd(0)
                store_x2(2)
                store_x2(3)
                with sp.Fori(1, FT - 1) as f:
                    for c in range(3):
                        next_idx(f, c)
                    store_wd(f)
                store_wd(FT - 1)
                sp.wait_ge(wd_stored, 16 * FT)
                sp.wait_ge(wlo_ready, 2 * FT)
                for f in range(FT):
                    if f >= 3:
                        sp.wait_ge(wdlo_ready, f - 2)
                    sp.dma_start(w32[:, f % 3, :], wd_scratch[f]).then_inc(wd_in[f % 3], 16)
                sp.wait_ge(x2_out, 16 * S)
                for t in range(TT + 2):
                    if t < TT:
                        if t >= RR:
                            sp.wait_ge(stored, (t - RR) * 16 + 16)
                        b, c = divmod(t, 4)
                        sp.dma_start(res[:, t % RR, :], x2_scratch[b, c * P:(c + 1) * P, :]).then_inc(x2_in, 16)
                        sp.wait_ge(x2_in, 16 * t + 16)
                    if t >= 2:
                        b, c = divmod(t - 2, 4)
                        sp.wait_ge(out_ready, t - 1)
                        sp.dma_start(out[b, c * P:(c + 1) * P, :], res[:, (t - 2) % RR, :]).then_inc(stored, 16)
                sp.wait_ge(stored, TT * 16)

            @block.tensor
            def _(pe):
                mm = nc.tensor.matmul

                def residual(b):
                    pe.wait_ge(x1_in[b], 16)
                    for lt in range(4):
                        if b:
                            pe.wait_ge(x2_ready, (b - 1) * 4 + lt + 1)
                        mm(banks[:, 2 + lt, :], ident[:], x1b[b][:, lt, :], start=True, stop=False)
                        if lt == 0:
                            pe.wait_ge(gated, b + 1)
                        for et in range(4):
                            last = mm(banks[:, 2 + lt, et * P:(et + 1) * P], yb[b][:, et, lt * P:(lt + 1) * P],
                                      ident[:], start=False, stop=et == 3)
                        last.then_inc(sum_out, 1)

                def x2_over(b):
                    pe.wait_ge(x2_ready, b * 4 + 4)
                    for ht in range(4):
                        if b:
                            pe.wait_ge(x2lo_ready, b * 4 + ht - (1 if b == 3 and ht >= 2 else 3))
                        for lt in range(4):
                            last = nc.tensor.transpose(banks[:, X2T_BANK(b, ht), lt * P:(lt + 1) * P],
                                                       x1b[b][:, lt, ht * P:(ht + 1) * P], ident[:])
                        last.then_inc(x2T_out, 1)

                def gate_up(f, par, blocks=range(TB), first=False):
                    pe.wait_ge(wlo_ready, f * 2 + 2)
                    for tb in blocks:
                        if first:
                            pe.wait_ge(x2lo_ready, 4 * tb + 4)
                            if tb == 0:
                                pe.wait_ge(x2lo_ready, 12)
                            elif tb < 3:
                                pe.wait_ge(x2_ready, 12 + 2 * tb)
                        else:
                            pe.wait_ge(h_ready, f * 4 - 3 + tb)
                        for w in range(2):
                            for t in range(HT):
                                for n, (ws, xs) in enumerate(((0, 0), (0, 1), (1, 0))):
                                    last = mm(banks[:, 2 * tb + w, :], wgu[:, par, w, ws, t * P:(t + 1) * P],
                                              x2T[:, xs, t, tb * 512:(tb + 1) * 512],
                                              start=t == 0 and n == 0, stop=t == HT - 1 and n == 2)
                        last.then_inc(gate_up_out, 1)

                for b in range(3):
                    residual(b)
                    x2_over(b)
                residual(3)
                gate_up(0, 0, (0,), first=True)
                x2_over(3)
                gate_up(0, 0, (1, 2, 3), first=True)
                with pe.Fori(1, FT - 1, 2) as f:
                    gate_up(f, 1)
                    gate_up(f + 1, 0)

                def down(bank, f, hi, lo):
                    rows = P if f < FT - 1 else FLAST
                    for n, (h, w) in enumerate(((hi, wd[0]), (hi, wd[1]), (lo, wd[0]))):
                        last = mm(banks[:, bank, :], h[0:rows], w[0:rows, f, :],
                                  start=f == 0 and n == 0, stop=f == FT - 1 and n == 2)
                    return last

                pe.wait_ge(h_ready, FT * 4)
                for f in range(FT):
                    pe.wait_ge(wdlo_ready, f + 1)
                    pe.wait_ge(hglo_ready, f + 1)
                    for t in range(GT):
                        last = down(t, f, *[hg[f % 2][s][:, t * P:(t + 1) * P] for s in range(2)])
                        if f == FT - 1:
                            last.then_inc(down_out, 1)
                    if f < FT - 1:
                        last.then_inc(group_step, 1)

                def four_tiles(t0, first=False):
                    for d in range(4):
                        pe.wait_ge(hlo_ready, t0 + d - GT + 1)
                        if not first:
                            pe.wait_ge(res_ready, t0 + d - 3)
                        for f in range(FT):
                            last = down(4 + d, f, h_hi[d % 2][:, f, :], h_lo[d % 2][:, f, :])
                        last.then_inc(down_out, 1)

                four_tiles(GT, first=True)
                with pe.Fori(2 * GT, TT - 3, 4) as t0:
                    four_tiles(t0)

            @block.scalar
            def _(act):
                A = nc.scalar.activation

                def gates(b):
                    act.wait_ge(x1_in[b], 16)
                    if b >= 2:
                        act.wait_ge(gated, b - 1)
                    A(gate[b % 2], x1b[b], ACT.Silu).then_inc(gate_ready, 1)

                def norm_apply(b):
                    act.wait_ge(shift_ready, b + 1)
                    for lt in range(4):
                        A(x1b[b][:, lt, :], banks[:, 2 + lt, :], ACT.Identity, bias=shift[:, lt:lt + 1],
                          scale=rstd[:, lt:lt + 1]).then_inc(x2_ready, 1)

                def x2T_hi(b):
                    for ht in range(HT):
                        act.wait_ge(x2T_out, b * 4 + ht + 1)
                        A(x2T[:, 0, ht, b * 512:(b + 1) * 512], banks[:, X2T_BANK(b, ht), :], ACT.Copy)\
                            .then_inc(x2hi_ready, 1)

                def leaves(f, c, par, js=range(7), first=False):
                    n7 = f * 21 + 7 * c
                    parity = (par + c) % 2
                    act.wait_ge(bits_ready, f * 9 + 3 * c + 1)
                    for j in js:
                        if j == 0:
                            if not first:
                                if c < 2:
                                    act.wait_ge(wlo_ready, f * 2 + c - 1)
                                else:
                                    act.wait_ge(wd_stored, f * 16)
                        elif j in LEAF_AFTER:
                            act.wait_ge(mux_ready, n7 + LEAF_AFTER[j])
                        elif not (first and c == 0):
                            act.wait_ge(mux_ready, n7 - 7 + LEAF_AFTER_LAST[j])
                        A(buffer(LEAF_ROLE[j], c, parity), bit0[:, parity, :], ACT.Identity,
                          bias=table[:, 2 * j:2 * j + 1], scale=table_gap[:, j:j + 1]).then_inc(leaf_ready, 1)
                        if j == 3 and c:
                            act.wait_ge(mux_ready, n7)
                            if not first and not isinstance(f, int) or isinstance(f, int) and f >= 2:
                                act.wait_ge(gate_up_out, f * 4 - 4)
                            A(wgu[:, par, c - 1, 0, :], w32[:, c - 1, :], ACT.Copy).then_inc(whi_ready, 1)

                def silus(f, tb):
                    act.wait_ge(gate_up_out, f * 4 + tb + 1)
                    if not isinstance(f, int) or f or tb >= 2:
                        act.wait_ge(h_ready, f * 4 + tb - 1)
                    A(silu[:, tb % 2, :], banks[:, 2 * tb, :], ACT.Silu).then_inc(silu_ready, 1)

                act.wait_ge(gap_ready, 1)
                early, late = range(4), range(4, 7)
                leaves(0, 0, 0, early, first=True)
                gates(0)
                leaves(0, 0, 0, late, first=True)
                gates(1)
                for b in range(S):
                    f, c = divmod(b + 1, 3)
                    leaves(f, c, f, early, first=f == 0)
                    norm_apply(b)
                    leaves(f, c, f, late, first=f == 0)
                    if b + 2 < S:
                        gates(b + 2)
                    x2T_hi(b)
                leaves(1, 2, 1)
                for tb in range(TB):
                    silus(0, tb)

                def tile(f, par):
                    for c in range(3):
                        leaves(f + 1, c, par)
                        silus(f, c)
                    silus(f, 3)

                with act.Fori(1, FT - 2, 2) as f:
                    tile(f, 0)
                    tile(f + 1, 1)
                tile(FT - 2, 0)
                for tb in range(TB):
                    silus(FT - 1, tb)

                act.wait_ge(h_ready, FT * 4)
                act.wait_ge(gate_up_out, FT * 4)
                for f in range(FT):
                    act.wait_ge(wd_in[f % 3], 16 * (f // 3 + 1))
                    A(wd[0][:, f, :], w32[:, f % 3, :], ACT.Copy).then_inc(wdhi_ready, 1)
                    if f >= 2:
                        act.wait_ge(group_step, f - 1)
                    A(hg[f % 2][0], hT[:, f, 0:GT * P], ACT.Copy).then_inc(hghi_ready, 1)
                for what, t in ORDER:
                    if what == "split":
                        if t >= GT + 2:
                            act.wait_ge(down_out, t - 1)
                        A(h_hi[t % 2], hT[:, :, t * P:(t + 1) * P], ACT.Copy).then_inc(hhi_ready, 1)
                    else:
                        act.wait_ge(shift4_ready, t + 1)
                        A(res[:, t % RR, :], res[:, t % RR, :], ACT.Identity, bias=shift[:, t % 4:t % 4 + 1],
                          scale=rstd[:, t % 4:t % 4 + 1]).then_inc(out_ready, 1)

            @block.vector
            def _(dve):
                V = nc.vector

                def take_bit(k, f, c, parity):
                    if k == 0:
                        dve.wait_ge(idx_in[c], f * 16 + 16)
                    else:
                        if not (isinstance(f, int) and f == 0 and c == 0):
                            dve.wait_ge(mux_ready, f * 21 + 7 * c - 7 + 4 + k)
                    dst = bits[:, k - 1, :] if k else bit0[:, parity, :]
                    V.tensor_scalar(dst, idx_sb[:, c, :], 1 << k, None, ALU.bitwise_and).then_inc(bits_ready, 1)

                def select(f, c, par, last=False):
                    parity = (par + c) % 2
                    f_next, c_next = (f, c + 1) if c < 2 else (f + 1, 0)
                    for m, (kept, other, bit) in enumerate(MUX):
                        dve.wait_ge(leaf_ready, f * 21 + 7 * c + MUX_LEAVES[m])
                        if m == 4:
                            dve.wait_ge(leaf7_ready, f * 3 + c + 1)
                        if m in MUX_AFTER:
                            dve.wait_ge(mux_ready, f * 21 + 7 * c + MUX_AFTER[m])
                        if bit == 3:
                            dve.wait_ge(top_ready, f * 3 + c + 1)
                        else:
                            dve.wait_ge(bits_ready, f * 9 + 3 * c + bit + 1)
                        V.memset(wait_here[:, m:m + 1], 0.0)
                        V.copy_predicated(buffer(kept, c, parity), bits[:, bit - 1, :], buffer(other, c, parity))\
                            .then_inc(mux_ready, 1)
                        if m >= 4 and not last:
                            take_bit(m - 4, f_next, c_next, 1 - parity)

                def norm_factors(b):
                    for lt in range(4):
                        dve.wait_ge(sum_out, b * 4 + lt + 1)
                        V.bn_stats(stats[:, lt, :], banks[:, 2 + lt, :]).then_inc(stat_ready, 1)
                    for lt in range(4):
                        dve.wait_ge(stat_ready, b * 4 + lt + 1)
                        V.bn_aggr(meanvar[:, lt, :], stats[:, lt, :]).then_inc(mv_ready, 1)
                    dve.wait_ge(mv_ready, b * 4 + 4)
                    V.tensor_scalar(vareps[:], meanvar[:, :, 1], EPS, None, ALU.add).then_inc(ve_ready, 1)
                    dve.wait_ge(rstd_ready, b + 1)
                    V.scalar_tensor_tensor(shift[:], meanvar[:, :, 0], -1.0, rstd[:], ALU.mult, ALU.mult)\
                        .then_inc(shift_ready, 1)

                def x2T_lo(b):
                    for ht in range(HT):
                        dve.wait_ge(x2hi_ready, b * 4 + ht + 1)
                        V.tensor_tensor(x2T[:, 1, ht, b * 512:(b + 1) * 512], banks[:, X2T_BANK(b, ht), :],
                                        x2T[:, 0, ht, b * 512:(b + 1) * 512].bitcast(f32), ALU.subtract)\
                            .then_inc(x2lo_ready, 1)

                dve.wait_ge(lut_in, 16)
                pairs = table[:].rearrange("p (j two) -> p j two", two=2)
                V.tensor_tensor(table_gap[:], pairs[:, :, 1], pairs[:, :, 0], ALU.subtract).then_inc(gap_ready, 1)
                for k in range(3):
                    take_bit(k, 0, 0, 0)
                select(0, 0, 0)
                for b in range(S):
                    norm_factors(b)
                    f, c = divmod(b + 1, 3)
                    select(f, c, f)
                    x2T_lo(b)
                select(1, 2, 1)

                def inner(f, tb):
                    dve.wait_ge(silu_ready, f * 4 + tb + 1)
                    V.tensor_tensor(hT[:, f, tb * 512:(tb + 1) * 512], silu[:, tb % 2, :],
                                    banks[:, 2 * tb + 1, :], ALU.mult).then_inc(h_ready, 1)

                def tile(f, par, last=False):
                    for c in range(3):
                        select(f + 1, c, par, last=last and c == 2)
                        inner(f, c)
                    inner(f, 3)

                dve.wait_ge(x2_out, 16 * S)
                for tb in range(TB):
                    inner(0, tb)
                with dve.Fori(1, FT - 2, 2) as f:
                    tile(f, 0)
                    tile(f + 1, 1)
                tile(FT - 2, 0, last=True)
                for tb in range(TB):
                    inner(FT - 1, tb)

                for f in range(FT):
                    dve.wait_ge(wdhi_ready, f + 1)
                    V.tensor_tensor(wd[1][:, f, :], w32[:, f % 3, :], wd[0][:, f, :].bitcast(f32), ALU.subtract)\
                        .then_inc(wdlo_ready, 1)
                    dve.wait_ge(hghi_ready, f + 1)
                    V.tensor_tensor(hg[f % 2][1], hT[:, f, 0:GT * P], hg[f % 2][0].bitcast(f32), ALU.subtract)\
                        .then_inc(hglo_ready, 1)

                for what, t in ORDER:
                    if what == "split":
                        dve.wait_ge(hhi_ready, t - GT + 1)
                        V.tensor_tensor(h_lo[t % 2], hT[:, :, t * P:(t + 1) * P], h_hi[t % 2].bitcast(f32),
                                        ALU.subtract).then_inc(hlo_ready, 1)
                        continue
                    r = res[:, t % RR, :]
                    j = t % 4
                    dve.wait_ge(down_out, t + 1)
                    dve.wait_ge(x2_in, 16 * t + 16)
                    V.tensor_tensor(r, banks[:, t if t < GT else 4 + t % 4, :], r, ALU.add).then_inc(res_ready, 1)
                    dve.wait_ge(res_ready, t + 1)
                    V.bn_stats(stats[:, j, :], r).then_inc(stat4_ready, 1)
                    dve.wait_ge(stat4_ready, t + 1)
                    V.bn_aggr(meanvar[:, j, :], stats[:, j, :]).then_inc(mv4_ready, 1)
                    dve.wait_ge(mv4_ready, t + 1)
                    V.tensor_scalar(vareps[:, j:j + 1], meanvar[:, j, 1:2], EPS, None, ALU.add)\
                        .then_inc(ve4_ready, 1)
                    dve.wait_ge(rstd4_ready, t + 1)
                    V.scalar_tensor_tensor(shift[:, j:j + 1], meanvar[:, j, 0:1], -1.0, rstd[:, j:j + 1],
                                           ALU.mult, ALU.mult).then_inc(shift4_ready, 1)

            @block.gpsimd
            def _(pool):
                G = nc.gpsimd

                def stage2_rstd(b):
                    pool.wait_ge(ve_ready, b + 1)
                    if b:
                        pool.wait_ge(x2_ready, 4 * b)
                    G.tensor_tensor(rstd[:], vareps[:], minus_half[:], ALU.pow).then_inc(rstd_ready, 1)

                def gate_y(b):
                    pool.wait_ge(gate_ready, b + 1)
                    pool.wait_ge(y_in[b], 16)
                    G.tensor_tensor(yb[b], yb[b], gate[b % 2], ALU.mult).then_inc(gated, 1)

                def top_and_leaf7(f, c, par):
                    parity = (par + c) % 2
                    pool.wait_ge(idx_in[c], f * 16 + 16)
                    if not (isinstance(f, int) and f == 0 and c == 0):
                        pool.wait_ge(mux_ready, f * 21 + 7 * c)
                    G.tensor_tensor(pool_wait_here[:, 0:1], minus_half[:, 0:1], minus_half[:, 0:1], ALU.add)
                    G.tensor_scalar(bits[:, 2, :], idx_sb[:, c, :], 8, None, ALU.is_ge).then_inc(top_ready, 1)
                    pool.wait_ge(bits_ready, f * 9 + 3 * c + 1)
                    G.tensor_tensor(pool_wait_here[:, 1:2], minus_half[:, 0:1], minus_half[:, 0:1], ALU.add)
                    G.tensor_scalar(buffer(4, c, parity), bit0[:, parity, :], table_gap[:, 7:8], table[:, 14:15],
                                    ALU.mult, ALU.add).then_inc(leaf7_ready, 1)

                def low_part(f, c, par):
                    if c:
                        pool.wait_ge(whi_ready, f * 2 + c)
                        G.tensor_tensor(wgu[:, par, c - 1, 1, :], w32[:, c - 1, :],
                                        wgu[:, par, c - 1, 0, :].bitcast(f32), ALU.subtract).then_inc(wlo_ready, 1)

                pool.wait_ge(gap_ready, 1)
                top_and_leaf7(0, 0, 0)
                gate_y(0)
                for b in range(S):
                    f, c = divmod(b + 1, 3)
                    top_and_leaf7(f, c, f)
                    if b == 0:
                        gate_y(1)
                    low_part(f, c, f)
                    stage2_rstd(b)
                    if b in (1, 2):
                        gate_y(b + 1)
                top_and_leaf7(1, 2, 1)
                low_part(1, 2, 1)

                def tile(f, par):
                    for c in range(3):
                        top_and_leaf7(f, c, par)
                        low_part(f, c, par)

                with pool.Fori(2, FT - 1, 2) as f:
                    tile(f, 0)
                    tile(f + 1, 1)
                tile(FT - 1, 0)
                for what, t in ORDER:
                    if what == "norm":
                        j = t % 4
                        pool.wait_ge(ve4_ready, t + 1)
                        if t >= 4:
                            pool.wait_ge(out_ready, t - 3)
                        G.tensor_tensor(rstd[:, j:j + 1], vareps[:, j:j + 1], minus_half[:, j:j + 1], ALU.pow)\
                            .then_inc(rstd4_ready, 1)


def kernel(**inputs):
    import numpy as np
    import ml_dtypes
    import concourse.bacc as bacc
    from concourse.bass_utils import run_bass_kernel_spmd

    def arr(name):
        return np.asarray(inputs[name])

    x = arr("x")
    wqkv = arr("L0_attn_weight_qkv").reshape(4, QT + 2, HD, H)
    wp = arr("L0_attn_weight_proj").reshape(H, 4, QT, HD)
    per_channel = np.concatenate([
        arr("L0_xattn_conv_w"), arr("L0_xattn_conv_b")[:, None], arr("L0_xattn_dt_proj_b")[:, None],
        arr("L0_xattn_D")[:, None], arr("L0_xattn_A_log")], axis=1)
    xp = arr("L0_xattn_x_proj_w")

    def tiles(w):
        return np.concatenate([w, w[:FT * P - F]], axis=0).reshape(FT, P, H)

    gate_up = [tiles(arr(n)).transpose(0, 2, 1).reshape(FT, HT, P, P).transpose(0, 2, 1, 3).reshape(FT, P, H)
               for n in ("L0_ffn_gate_idx", "L0_ffn_up_idx")]
    down = tiles(arr("L0_ffn_down_idx").T)

    rows = np.arange(P)
    headsum = np.zeros((P, QT, 32), np.float32)
    for qt in range(QT):
        headsum[rows, qt, 4 * qt + rows // HD] = 1
    spread = np.zeros((P, S * QT, P), np.float32)
    for i in range(S):
        for qt in range(QT):
            spread[32 * i + 4 * qt + rows // HD, i * QT + qt, rows] = 1
    pick = np.tile(np.eye(32), (3, 1)).astype(ml_dtypes.bfloat16)

    arrays = {
        "xT": x.transpose(2, 0, 1).reshape(H, S * L),
        "x": x,
        "ctxT": arr("ctx_1024").transpose(2, 0, 1).reshape(DM, S * L),
        "wqkvT": wqkv.transpose(1, 0, 2, 3).reshape(6 * P, H).T,
        "wpT": wp.transpose(2, 1, 3, 0).reshape(H, H),
        "ipT": arr("L0_xattn_in_proj_w").T,
        "chan": per_channel.reshape(ET, P, -1).transpose(1, 0, 2),
        "xpT": np.concatenate([xp[DR:], xp[:DR]], axis=0).T,
        "dtT": arr("L0_xattn_dt_proj_w").T,
        "lut": arr("L0_ffn_lut").reshape(1, 16),
        "idx": np.concatenate(gate_up + [down], axis=2),
        "ident_c": np.eye(P, dtype=np.float32),
        "headsum_c": headsum,
        "spread_c": spread,
        "pick_c": pick,
    }
    nc = bacc.Bacc("TRN2", target_bir_lowering=False, num_devices=1)
    args = {}
    for name, a in arrays.items():
        a = arrays[name] = np.ascontiguousarray(a)
        args[name] = nc.dram_tensor(f"in_{name}", a.shape, mybir.dt.from_np(a.dtype), kind="ExternalInput").ap()
    out = nc.dram_tensor("out_0", (S, L, H), mybir.dt.float32, kind="ExternalOutput").ap()
    decoder_kernel(nc, out=out, **args)
    r = run_bass_kernel_spmd(nc, [{f"in_{n}": a for n, a in arrays.items()}], core_ids=[0])
    return r.results[0]["out_0"]
```
